# Optimizing a Trainium2 kernel written in Bass

```python
import numpy as np
import jax
import jax.numpy as jnp

def _softmax(x, axis=-1):
    return jax.nn.softmax(x, axis=axis)

def _gelu(x):
    return jax.nn.gelu(x, approximate=True)

def _silu(x):
    return jax.nn.silu(x)

def _sigmoid(x):
    return jax.nn.sigmoid(x)

def _layernorm(x, axis=-1, eps=1e-05):
    m = jnp.mean(x, axis=axis, keepdims=True)
    v = jnp.var(x, axis=axis, keepdims=True)
    return (x - m) / jnp.sqrt(v + eps)

def _scatter_add(tgt, idx, src, axis=0):
    return tgt.at[idx].add(src)

def _segment_sum(src, seg, n):
    return jax.ops.segment_sum(src, seg, n)
kernel_name = 'mk_gnn_resnorm_d2_gnn_r64_b58003'

def setup_inputs(seed: int=0):
    np.random.seed(seed)
    _w = jnp.asarray

    def _rec_inputs():
        import jax
        import jax.numpy as jnp
        _gk = jax.random.key(seed)
        x = -0.0003713 + 1 * jax.random.normal(jax.random.fold_in(_gk, 1), (50000, 128), jnp.float32)
        src = jax.random.randint(jax.random.fold_in(_gk, 2), (25000,), 0, 50000, jnp.int32)
        dst = jax.random.randint(jax.random.fold_in(_gk, 3), (25000,), 0, 50000, jnp.int32)
        _o = jnp.argsort(dst, stable=True)
        src = src[_o]
        dst = dst[_o]
        edge_attr_64 = 0.000167468 + 1.0002 * jax.random.normal(jax.random.fold_in(_gk, 12), (25000, 64), jnp.float32)
        edge_type_4 = jax.random.randint(jax.random.fold_in(_gk, 14), (25000,), 0, 4, jnp.int32)
        return (x, src, dst, edge_attr_64, edge_type_4)
    x, src, dst, edge_attr_64, edge_type_4 = _rec_inputs()

    def _L0_gnn_setup():
        import jax, jax.numpy as jnp
        import numpy as np
        N = 100000
        E = 10000
        WIDTH = 128
        NUM_FEATURES = 64

        def _linear_relu(h, W, b):
            return jax.nn.relu(h @ W + b)
        key = jax.random.key(seed)
        k = jax.random.split(key, 8)
        x = jax.random.normal(k[0], (N, WIDTH), dtype=jnp.float32)
        e = jax.random.randint(k[1], (2, E), 0, N, dtype=jnp.int32)
        e_feat = jax.random.normal(k[2], (E, NUM_FEATURES), dtype=jnp.float32)
        s_e = 1.0 / np.sqrt(WIDTH + NUM_FEATURES)
        s_m = 1.0 / np.sqrt(2 * WIDTH)
        W_edge = jax.random.uniform(k[3], (WIDTH + NUM_FEATURES, WIDTH), jnp.float32, -s_e, s_e)
        b_edge = jax.random.uniform(k[4], (WIDTH,), jnp.float32, -s_e, s_e)
        W_mlp = jax.random.uniform(k[5], (2 * WIDTH, WIDTH), jnp.float32, -s_m, s_m)
        b_mlp = jax.random.uniform(k[6], (WIDTH,), jnp.float32, -s_m, s_m)
        return {'x': x, 'e': e, 'e_feat': e_feat, 'W_edge': W_edge, 'b_edge': b_edge, 'W_mlp': W_mlp, 'b_mlp': b_mlp}
    _L0_gnn_all = _L0_gnn_setup()
    _L0_gnn_in = {k: v for k, v in _L0_gnn_all.items() if k in ('W_edge', 'b_edge', 'W_mlp', 'b_mlp')}
    del _L0_gnn_all

    def _L1_gnn_setup():
        import jax, jax.numpy as jnp
        import numpy as np
        N = 100000
        E = 25000
        D = 128
        G = 128
        K = 4
        STEPS = 3

        def _gru_cell(a, h, W_ih, b_ih, W_hh, b_hh):
            gi = a @ W_ih.T + b_ih
            gh = h @ W_hh.T + b_hh
            ir, iz, in_ = jnp.split(gi, 3, axis=1)
            hr, hz, hn = jnp.split(gh, 3, axis=1)
            r = jax.nn.sigmoid(ir + hr)
            z = jax.nn.sigmoid(iz + hz)
            n = jnp.tanh(in_ + r * hn)
            return (1.0 - z) * n + z * h
        key = jax.random.key(seed)
        ks = jax.random.split(key, 16)
        s = 0.05
        return {'features': jax.random.normal(ks[0], (N, D), jnp.float32), 'src': jax.random.randint(ks[1], (E,), 0, N, jnp.int32), 'dst': jax.random.randint(ks[2], (E,), 0, N, jnp.int32), 'etypes': jax.random.randint(ks[3], (E,), 0, K, jnp.int32), 'W_et': jax.random.normal(ks[4], (K, D, D), jnp.float32) * s, 'b_et': jax.random.normal(ks[5], (K, D), jnp.float32) * s, 'W_ih': jax.random.normal(ks[6], (3 * D, D), jnp.float32) * s, 'b_ih': jax.random.normal(ks[7], (3 * D,), jnp.float32) * s, 'W_hh': jax.random.normal(ks[8], (3 * D, D), jnp.float32) * s, 'b_hh': jax.random.normal(ks[9], (3 * D,), jnp.float32) * s, 'i_w': jax.random.normal(ks[10], (G, D + D), jnp.float32) * s, 'i_b': jax.random.normal(ks[11], (G,), jnp.float32) * s, 'j_w': jax.random.normal(ks[12], (G, D), jnp.float32) * s, 'j_b': jax.random.normal(ks[13], (G,), jnp.float32) * s}
    _L1_gnn_all = _L1_gnn_setup()
    _L1_gnn_in = {k: v for k, v in _L1_gnn_all.items() if k in ('W_et', 'b_et', 'W_ih', 'b_ih', 'W_hh', 'b_hh', 'i_w', 'i_b', 'j_w', 'j_b')}
    del _L1_gnn_all
    return {'x': x, 'src': src, 'dst': dst, 'edge_attr_64': edge_attr_64, 'edge_type_4': edge_type_4, 'L0_gnn_W_edge': _L0_gnn_in['W_edge'], 'L0_gnn_b_edge': _L0_gnn_in['b_edge'], 'L0_gnn_W_mlp': _L0_gnn_in['W_mlp'], 'L0_gnn_b_mlp': _L0_gnn_in['b_mlp'], 'L1_gnn_W_et': _L1_gnn_in['W_et'], 'L1_gnn_b_et': _L1_gnn_in['b_et'], 'L1_gnn_W_ih': _L1_gnn_in['W_ih'], 'L1_gnn_b_ih': _L1_gnn_in['b_ih'], 'L1_gnn_W_hh': _L1_gnn_in['W_hh'], 'L1_gnn_b_hh': _L1_gnn_in['b_hh'], 'L1_gnn_i_w': _L1_gnn_in['i_w'], 'L1_gnn_i_b': _L1_gnn_in['i_b'], 'L1_gnn_j_w': _L1_gnn_in['j_w'], 'L1_gnn_j_b': _L1_gnn_in['j_b']}

def reference(x, src, dst, edge_attr_64, edge_type_4, L0_gnn_W_edge, L0_gnn_b_edge, L0_gnn_W_mlp, L0_gnn_b_mlp, L1_gnn_W_et, L1_gnn_b_et, L1_gnn_W_ih, L1_gnn_b_ih, L1_gnn_W_hh, L1_gnn_b_hh, L1_gnn_i_w, L1_gnn_i_b, L1_gnn_j_w, L1_gnn_j_b):
    import jax
    import jax.numpy as jnp

    def _L0_gnn_ref(x, e, e_feat, W_edge, b_edge, W_mlp, b_mlp):
        import jax, jax.numpy as jnp
        import numpy as np
        N = 100000
        E = 10000
        WIDTH = 128
        NUM_FEATURES = 64

        def _linear_relu(h, W, b):
            return jax.nn.relu(h @ W + b)
        src, dst = (e[0], e[1])
        diffs = x[dst] - x[src]
        ef = diffs + _linear_relu(jnp.concatenate([diffs, e_feat], axis=1), W_edge, b_edge)
        maxes = jax.ops.segment_max(ef, dst, num_segments=x.shape[0])
        maxes = jnp.where(jnp.isneginf(maxes), 0.0, maxes)
        return x + _linear_relu(jnp.concatenate([x, maxes], axis=1), W_mlp, b_mlp)

    def _L1_gnn_ref(features, src, dst, etypes, W_et, b_et, W_ih, b_ih, W_hh, b_hh, i_w, i_b, j_w, j_b):
        import jax, jax.numpy as jnp
        import numpy as np
        N = 100000
        E = 25000
        D = 128
        G = 128
        K = 4
        STEPS = 3

        def _gru_cell(a, h, W_ih, b_ih, W_hh, b_hh):
            gi = a @ W_ih.T + b_ih
            gh = h @ W_hh.T + b_hh
            ir, iz, in_ = jnp.split(gi, 3, axis=1)
            hr, hz, hn = jnp.split(gh, 3, axis=1)
            r = jax.nn.sigmoid(ir + hr)
            z = jax.nn.sigmoid(iz + hz)
            n = jnp.tanh(in_ + r * hn)
            return (1.0 - z) * n + z * h
        n_nodes = features.shape[0]
        h = features
        for _ in range(STEPS):
            t = jnp.einsum('nd,kod->kno', h, W_et) + b_et[:, None, :]
            msg = t[etypes, src]
            a = jax.ops.segment_sum(msg, dst, num_segments=n_nodes)
            h = _gru_cell(a, h, W_ih, b_ih, W_hh, b_hh)
        gate = jax.nn.sigmoid(jnp.concatenate([h, features], axis=1) @ i_w.T + i_b)
        return gate * (h @ j_w.T + j_b)
    edge_index = jnp.stack([src, dst])
    x = _layernorm(x + _L0_gnn_ref(x, edge_index, edge_attr_64, L0_gnn_W_edge, L0_gnn_b_edge, L0_gnn_W_mlp, L0_gnn_b_mlp), axis=-1)
    x = _layernorm(x + _L1_gnn_ref(x, src, dst, edge_type_4, L1_gnn_W_et, L1_gnn_b_et, L1_gnn_W_ih, L1_gnn_b_ih, L1_gnn_W_hh, L1_gnn_b_hh, L1_gnn_i_w, L1_gnn_i_b, L1_gnn_j_w, L1_gnn_j_b), axis=-1)
    return x

_drawn_inputs = setup_inputs


def setup_inputs(seed=0):
    import zlib

    import numpy as np

    out = dict(_drawn_inputs(seed))
    spreads = {}
    factors = {'edge_attr_64': 3.017,
     'L0_gnn_b_edge': 22.206,
     'L0_gnn_b_mlp': 4.363,
     'L1_gnn_b_et': 8.0,
     'L1_gnn_b_ih': 4.786,
     'L1_gnn_b_hh': 7.693,
     'L1_gnn_i_w': 3.319,
     'L1_gnn_i_b': 33.067}
    for name, (base, spread) in spreads.items():
        noise = np.random.default_rng([zlib.crc32(name.encode()), seed]).standard_normal(out[name].shape)
        drawn = base * np.exp(spread * noise) if base else spread * noise
        out[name] = jnp.asarray(drawn.astype(out[name].dtype))
    for name, factor in factors.items():
        out[name] = (out[name] * factor).astype(out[name].dtype)
    return out
```

```python
from contextlib import ExitStack

import concourse.bass as bass
from concourse import mybir

P = 128
N = 50000
E = 25000
CH = 4
TILE = P * CH
ET = -(-E // TILE)
EPAD = ET * TILE
NT = -(-N // TILE)
NPAD = NT * TILE
ECOL = EPAD // P
KT = 4
F_E = 64
STEPS = 3
STREAMS = 2
NOWHERE = 1 << 20
LN_EPS = 1e-5
RESTART = -3.0e38
assert NT == STREAMS * ET

ALU = mybir.AluOpType
ACT = mybir.ActivationFunctionType
F32 = mybir.dt.float32
BF16 = mybir.dt.bfloat16
I32 = mybir.dt.int32
U8 = mybir.dt.uint8

W_NAMES = (["edge_x", "edge_f", "mlp_x", "mlp_m"] + [f"et{k}" for k in range(KT)]
           + ["ih_r", "ih_z", "ih_n", "hh_r", "hh_z", "hh_n", "i_h", "i_x", "j"])
B_NAMES = ["edge"] + [f"et{k}" for k in range(KT)] + ["ih_r", "ih_z", "ih_n", "hh_r", "hh_z", "hh_n"]
R_NAMES = ["mlp", "i", "j"] + [f"et{k}" for k in range(KT)]


def build(nc, x, dst_lin, prev_lin, type_lin, dst_t, next_t, src_t, ef_t, weights, biases, bias_rows, out):
    with ExitStack() as ctx:
        def sb(name, shape, dt=F32):
            return ctx.enter_context(nc.sbuf_tensor(name, shape, dt))

        def sem(name):
            return ctx.enter_context(nc.semaphore(name))

        def sems(name, n=STREAMS):
            return [sem(f"{name}{k}") for k in range(n)]

        def dram(name, shape, dt=F32):
            return nc.dram_tensor(name, shape, dt, kind="Internal").ap()

        tables = [dram(f"table{s}", (NPAD + EPAD, P)) for s in range(STEPS)]
        states = [dram(f"state{s}", (ET, P, TILE)) for s in range(STEPS)]
        where = dram("where", (NPAD, 1), I32)
        src_rows = dram("src_rows", (ET, P, CH), I32)
        last_t = dram("last_t", (ET, P, CH), I32)
        rows_t = dram("rows_t", (ET, P, CH), I32)
        same_d = dram("same_d", (1, EPAD), BF16)
        restart_d = dram("restart_d", (1, EPAD), BF16)
        mask_d = dram("mask_d", (KT - 1, EPAD), U8)

        wt = sb("wt", [P, len(W_NAMES) * P])
        bs = sb("bs", [P, len(B_NAMES)])
        brz = sb("brz", [P, 2])
        brow = sb("brow", [1, len(R_NAMES) * P])
        bres = sb("bres", [1, len(R_NAMES) * P])
        bpart = [sb(f"bpart{k}", [1, len(R_NAMES) * P], BF16) for k in range(3)]
        ones = sb("ones", [1, TILE], BF16)
        ident = sb("ident", [P, P])
        half = sb("half", [P, CH])

        def w(name, rows=P):
            k = W_NAMES.index(name)
            return wt[0:rows, k * P:(k + 1) * P]

        def b(name):
            k = B_NAMES.index(name)
            return bs[:, k:k + 1]

        b_r, b_z = brz[:, 0:1], brz[:, 1:2]

        passed, v_passed, sp_passed = sem("passed"), sem("v_passed"), sem("sp_passed")

        banks = [ctx.enter_context(nc.psum_tensor(f"bank{k}", [P, TILE], F32)) for k in range(8)]

        def product(o, name, operand, first, last, rows=P):
            return nc.tensor.matmul(o, w(name, rows), operand, start=first, stop=last)

        def bias_into(o, name, lhs_rows, first, last):
            k = R_NAMES.index(name)
            for n in range(3):
                mm = nc.tensor.matmul(o, ones[:, 0:lhs_rows], bpart[n][:, k * P:(k + 1) * P],
                                      start=first and n == 0, stop=last and n == 2)
            return mm

        def bias_cols(o, name):
            k = R_NAMES.index(name)
            for n in range(3):
                mm = nc.tensor.matmul(o, bpart[n][:, k * P:(k + 1) * P], ones[:, :], start=False, stop=n == 2)
            return mm

        def flip(o, rows):
            for c in range(CH):
                mm = nc.tensor.transpose(o[:, c * P:(c + 1) * P], rows[:, c, :], ident[:, :])
            return mm

        def chunks(t):
            return t.rearrange("p (c f) -> p c f", c=CH)

        def row_product(bank, terms, bias):
            for c in range(CH):
                o = bank[:, c * P:(c + 1) * P]
                for n, (operand, name) in enumerate(terms):
                    nc.tensor.matmul(o, operand[:, c * P:(c + 1) * P], w(name), start=n == 0, stop=False)
                mm = bias_into(o, bias, P, False, True)
            return mm

        with ExitStack() as own:
            def sbo(name, shape, dt=I32):
                return own.enter_context(nc.sbuf_tensor(name, shape, dt))

            dl, pl, tl = sbo("dl", [P, ECOL]), sbo("pl", [P, ECOL]), sbo("tl", [P, ECOL])
            dt_, nt_ = sbo("dt_", [P, ECOL]), sbo("nt_", [P, ECOL])
            same_s, restart_s = sbo("same_s", [P, ECOL], BF16), sbo("restart_s", [P, ECOL], BF16)
            mask_s = sbo("mask_s", [P, KT - 1, ECOL], U8)
            more = sbo("more", [P, ECOL])
            last_s, rows_s, where_s = sbo("last_s", [P, ECOL]), sbo("rows_s", [P, ECOL]), sbo("where_s", [P, NPAD // P])
            loaded, ident_zero, pool_ready = sem("loaded"), sem("ident_zero"), sem("pool_ready")
            part, flags_ready = sem("part"), sem("flags_ready")
            setup_stored = sem("setup_stored")

            with nc.Block() as block:
                @block.sync
                def _(sp):
                    sp.dma_start(wt[:, :], weights).then_inc(loaded, 16)
                    sp.dma_start(bs[:, :], biases).then_inc(loaded, 16)
                    sp.dma_start(brow[:, :], bias_rows).then_inc(loaded, 16)
                    for t, d in ((dl, dst_lin), (pl, prev_lin), (tl, type_lin)):
                        sp.dma_start(t[:, :], d).then_inc(loaded, 16)
                    for t, d in ((dt_, dst_t), (nt_, next_t)):
                        sp.dma_start(t[:, :].rearrange("p (t c) -> p t c", c=CH),
                                     d.rearrange("t p c -> p t c")).then_inc(loaded, 16)
                    sp.wait_ge(pool_ready, 4)
                    sp.dma_start(where.rearrange("(p c) o -> p (c o)", p=P), where_s[:, :]).then_inc(setup_stored, 16)
                    sp.dma_start(rows_t.rearrange("t p c -> p t c"),
                                 rows_s[:, :].rearrange("p (t c) -> p t c", c=CH)).then_inc(setup_stored, 16)
                    sp.wait_ge(flags_ready, 1)
                    sp.dma_start(last_t.rearrange("t p c -> p t c"),
                                 last_s[:, :].rearrange("p (t c) -> p t c", c=CH)).then_inc(setup_stored, 16)
                    sp.dma_start(same_d.rearrange("o (p c) -> (o p) c", p=P), same_s[:, :]).then_inc(setup_stored, 16)
                    sp.dma_start(restart_d.rearrange("o (p c) -> (o p) c", p=P), restart_s[:, :]).then_inc(setup_stored, 16)
                    sp.dma_start(mask_d.rearrange("k (p c) -> p k c", p=P), mask_s[:, :, :]).then_inc(setup_stored, 16)
                    sp.wait_ge(setup_stored, 96)

                @block.gpsimd
                def _(pool):
                    nc.gpsimd.memset(ident[:, :], 0.0).then_inc(ident_zero, 1)
                    pool.wait_ge(ident_zero, 1)
                    nc.gpsimd.affine_select(out=ident[:, :], in_=ident[:, :], compare_op=ALU.not_equal, fill=1.0,
                                            base=0, pattern=[[-1, P]], channel_multiplier=1).then_inc(pool_ready, 1)
                    nc.gpsimd.memset(half[:, :], -0.5).then_inc(pool_ready, 1)
                    nc.gpsimd.iota(where_s[:, :], pattern=[[1, NPAD // P]], base=0,
                                   channel_multiplier=NPAD // P).then_inc(pool_ready, 1)
                    nc.gpsimd.iota(rows_s[:, :], pattern=[[P, ECOL]], base=NPAD,
                                   channel_multiplier=1).then_inc(pool_ready, 1)

                @block.vector
                def _(v):
                    v.wait_ge(loaded, 128)
                    made = [0]

                    def made_by(ins):
                        made[0] += 1
                        ins.then_inc(part, 1)

                    nc.vector.memset(ones[:, :], 1.0)
                    made_by(nc.vector.tensor_tensor(brz[:, 0:1], b("ih_r"), b("hh_r"), ALU.add))
                    made_by(nc.vector.tensor_tensor(brz[:, 1:2], b("ih_z"), b("hh_z"), ALU.add))
                    for n in range(3):
                        from_ = brow if n == 0 else bres
                        v.wait_ge(part, made[0])
                        made_by(nc.vector.tensor_copy(bpart[n][:, :], from_[:, :]))
                        v.wait_ge(part, made[0])
                        made_by(nc.vector.tensor_tensor(bres[:, :], from_[:, :], bpart[n][:, :], ALU.subtract))
                    made_by(nc.vector.tensor_tensor(same_s[:, :], dl[:, :], pl[:, :], ALU.is_equal))
                    v.wait_ge(part, made[0])
                    made_by(nc.vector.tensor_scalar(restart_s[:, :], same_s[:, :], -1.0, -RESTART, ALU.add, ALU.mult))
                    for k in range(1, KT):
                        made_by(nc.vector.tensor_scalar(mask_s[:, k - 1, :], tl[:, :], float(k), None, ALU.is_equal))
                    made_by(nc.vector.tensor_tensor(more[:, :], dt_[:, :], nt_[:, :], ALU.is_equal))
                    v.wait_ge(part, made[0])
                    nc.vector.scalar_tensor_tensor(last_s[:, :], more[:, :], float(NOWHERE), dt_[:, :],
                                                   ALU.mult, ALU.add).then_inc(flags_ready, 1)

        with ExitStack() as own:
            def sbo(name, shape, dt=F32):
                return own.enter_context(nc.sbuf_tensor(name, shape, dt))

            def pair(name, shape, dt=F32):
                return [sbo(f"{name}{u}", shape, dt) for u in range(STREAMS)]

            rows = [P, CH, P]
            cols = [P, TILE]
            xr, xT, relu_, y, x1r, x1T = (pair(n, s) for n, s in (
                ("xr", rows), ("xT", cols), ("relu_", rows), ("y", rows), ("x1r", rows), ("x1T", cols)))
            r_, z_, n_, t1_, zh_, m_, h_ = (pair(n, cols) for n in ("r_", "z_", "n_", "t1_", "zh_", "m_", "h_"))
            hr_, gate_, fin_, yo_, or_ = (pair(n, rows) for n in ("hr_", "gate_", "fin_", "yo_", "or_"))
            st_, mv_, ve_, rs_ = (pair(n, s) for n, s in (
                ("st_", [P, CH, 6]), ("mv_", [P, CH, 2]), ("ve_", [P, CH]), ("rs_", [P, CH])))
            eidx, lidx = sbo("eidx", [P, 2, CH], I32), sbo("lidx", [P, 2, CH], I32)
            xd, xs, df = sbo("xd", rows), sbo("xs", rows), sbo("df", rows)
            dfT, xdT, erelu, ef, emax = (sbo(n, cols) for n in ("dfT", "xdT", "erelu", "ef", "emax"))
            efT, restart = sbo("efT", [F_E, TILE]), sbo("restart", cols, BF16)
            carry = sbo("carry", [P, 1])
            emlp, ey, ex1r, ex1T = sbo("emlp", rows), sbo("ey", rows), sbo("ex1r", rows), sbo("ex1T", cols)
            est, emv, eve, ers = sbo("est", [P, CH, 6]), sbo("emv", [P, CH, 2]), sbo("eve", [P, CH]), sbo("ers", [P, CH])

            gate_bank = [[banks[3 * u + k] for k in range(3)] for u in range(STREAMS)]
            misc = [banks[6], banks[7]]
            USES = [["xT", "dfT", "mlp", "pre", "x1T", "h1", "h2"],
                    ["xT", "xdT", "mlp", "x1T", "emlp", "h1", "ex1T", "h2"]]
            misc_full = sems("misc_full")

            x_loaded = sems("x_loaded")
            xT_ready, relu_ready, y_ready = sems("xT_ready"), sems("relu_ready"), sems("y_ready")
            st_ready, mv_ready, ve_ready, rs_ready = sems("st_ready"), sems("mv_ready"), sems("ve_ready"), sems("rs_ready")
            x1_ready, x1T_ready, x1_stored = sems("x1_ready"), sems("x1T_ready"), sems("x1_stored")
            r_full, hn_full, z_full = sems("r_full"), sems("hn_full"), sems("z_full")
            r_ready, z_ready, n_ready = sems("r_ready"), sems("z_ready"), sems("n_ready")
            t1_ready, zh_ready, m_ready, h_ready = sems("t1_ready"), sems("zh_ready"), sems("m_ready"), sems("h_ready")
            hr_ready, hr_stored = sems("hr_ready"), sems("hr_stored")
            fin_full, gate_ready, fin_ready, yo_ready = sems("fin_full"), sems("gate_ready"), sems("fin_ready"), sems("yo_ready")
            out_ready, out_stored = sems("out_ready"), sems("out_stored")
            e_idx, e_gathered, l_idx, l_scattered = (sem(n) for n in (
                "e_idx", "e_gathered", "l_idx", "l_scattered"))
            df_ready, dfT_ready, xdT_ready, e_aux, pre_ready = (sem(n) for n in (
                "df_ready", "dfT_ready", "xdT_ready", "e_aux", "pre_ready"))
            ef_ready, emax_ready, carry_ready = (sem(n) for n in ("ef_ready", "emax_ready", "carry_ready"))
            e_stat, ve_e, rs_e = sem("e_stat"), sem("ve_e"), sem("rs_e")
            emlp_ready, ey_ready, ex1_ready, ex1T_ready, ex1_stored = (sem(n) for n in (
                "emlp_ready", "ey_ready", "ex1_ready", "ex1T_ready", "ex1_stored"))

            def use(m, name, i):
                return len(USES[m]) * i + USES[m].index(name)

            def node_rows(table, t):
                return table[bass.ds(t * TILE, TILE), :].rearrange("(p c) f -> p c f", c=CH)

            def edge_rows(table, t):
                return table[bass.ds(t * TILE + NPAD, TILE), :].rearrange("(c p) f -> p c f", p=P)

            with nc.Block() as block:
                @block.sync
                def _(sp):
                    def tile_of(a, i):
                        return a[bass.ds(i, 1), :, :].rearrange("t p c -> (t p) c")

                    def load_rows(i):
                        for u in range(STREAMS):
                            sp.wait_ge(y_ready[u], i)
                            sp.dma_start(xr[u][:, :, :], node_rows(x, i * STREAMS + u)).then_inc(x_loaded[u], 16)
                        sp.wait_ge(e_gathered, 128 * i)
                        sp.dma_start(eidx[:, 0, :], tile_of(dst_t, i)).then_inc(e_idx, 16)
                        sp.dma_start(eidx[:, 1, :], tile_of(src_t, i)).then_inc(e_idx, 16)
                        sp.wait_ge(pre_ready, i)
                        sp.dma_start(efT[:, :], ef_t[:, bass.ds(i * TILE, TILE)]).then_inc(e_aux, 16)
                        sp.wait_ge(emax_ready, i)
                        sp.sem_inc(sp_passed, 1)
                        sp.dma_start(restart[:, :], restart_d[:, bass.ds(i * TILE, TILE)].to_broadcast([P, TILE])).then_inc(e_aux, 16)

                    def load_last(i):
                        sp.wait_ge(l_scattered, 64 * i)
                        sp.dma_start(lidx[:, 0, :], tile_of(last_t, i)).then_inc(l_idx, 16)
                        sp.dma_start(lidx[:, 1, :], tile_of(rows_t, i)).then_inc(l_idx, 16)

                    def store_h(i, s, u):
                        sp.wait_ge(hr_ready[u], 2 * i + s + 1)
                        sp.dma_start(node_rows(tables[s + 1], i * STREAMS + u), hr_[u][:, :, :]).then_inc(hr_stored[u], 16)

                    def tiles(i, loads_next):
                        for u in range(STREAMS):
                            sp.wait_ge(x1_ready[u], i + 1)
                            sp.dma_start(node_rows(tables[0], i * STREAMS + u), x1r[u][:, :, :]).then_inc(x1_stored[u], 16)
                        if loads_next:
                            load_rows(i + 1)
                        store_h(i, 0, 0)
                        store_h(i, 0, 1)
                        sp.wait_ge(ex1T_ready, i + 1)
                        sp.dma_start(edge_rows(tables[0], i), ex1r[:, :, :]).then_inc(ex1_stored, 16)
                        sp.dma_start(tile_of(states[0], i), ex1T[:, :]).then_inc(ex1_stored, 16)
                        store_h(i, 1, 0)
                        store_h(i, 1, 1)
                        if loads_next:
                            load_last(i + 1)
                        for u in range(STREAMS):
                            sp.wait_ge(out_ready[u], i + 1)
                            sp.dma_start(node_rows(out, i * STREAMS + u), or_[u][:, :, :]).then_inc(out_stored[u], 16)

                    load_rows(0)
                    load_last(0)
                    with sp.Fori(0, ET - 1) as i:
                        tiles(i, True)
                    tiles(ET - 1, False)
                    for u in range(STREAMS):
                        sp.wait_ge(x1_stored[u], 16 * ET)
                        sp.wait_ge(hr_stored[u], 32 * ET)
                        sp.wait_ge(out_stored[u], 16 * ET)
                    sp.wait_ge(ex1_stored, 32 * ET)

                @block.gpsimd
                def _(pool):
                    def rstd(ve_done, value, ve, rs, ready):
                        pool.wait_ge(ve_done, value)
                        nc.gpsimd.tensor_tensor(rs[:, :], ve[:, :], half[:, :], ALU.pow).then_inc(ready, 1)

                    def keep(u, i, s):
                        pool.wait_ge(z_ready[u], 3 * i + s + 1)
                        pool.wait_ge(h_ready[u], 3 * i + s)
                        h = x1T[u] if s == 0 else h_[u]
                        nc.gpsimd.tensor_tensor(zh_[u][:, :], z_[u][:, :], h[:, :], ALU.mult).then_inc(zh_ready[u], 1)

                    def gather(i, ks):
                        pool.wait_ge(ey_ready, i)
                        pool.wait_ge(e_idx, 32 * i + 32)
                        pool.sem_inc(passed, 1)
                        for k in ks:
                            t, c = (xd, xs)[k // CH], k % CH
                            nc.gpsimd.indirect_dma_start(
                                out=t[:, c, :], out_offset=None, in_=x[:, :],
                                in_offset=bass.IndirectOffsetOnAxis(ap=eidx[:, k // CH, c:c + 1], axis=0),
                                bounds_check=NPAD - 1, oob_is_err=False).then_inc(e_gathered, 16)

                    def locate(i, c):
                        pool.wait_ge(l_idx, 32 * i + 32)
                        pool.sem_inc(passed, 1)
                        nc.gpsimd.indirect_dma_start(
                            out=where[:, :], out_offset=bass.IndirectOffsetOnAxis(ap=lidx[:, 0, c:c + 1], axis=0),
                            in_=lidx[:, 1, c:c + 1], in_offset=None,
                            bounds_check=NPAD - 1, oob_is_err=False).then_inc(l_scattered, 16)

                    def tiles(i, gathers_next):
                        for u in range(STREAMS):
                            rstd(ve_ready[u], 2 * i + 1, ve_[u], rs_[u], rs_ready[u])
                        locate(i, 0)
                        keep(0, i, 0)
                        locate(i, 1)
                        keep(1, i, 0)
                        rstd(ve_e, i + 1, eve, ers, rs_e)
                        locate(i, 2)
                        keep(0, i, 1)
                        locate(i, 3)
                        if gathers_next:
                            gather(i + 1, (0, 1))
                        keep(1, i, 1)
                        if gathers_next:
                            gather(i + 1, (4, 5))
                        keep(0, i, 2)
                        if gathers_next:
                            gather(i + 1, (2, 3))
                        keep(1, i, 2)
                        if gathers_next:
                            gather(i + 1, (6, 7))
                        for u in range(STREAMS):
                            rstd(ve_ready[u], 2 * i + 2, ve_[u], rs_[u], rs_ready[u])

                    gather(0, range(2 * CH))
                    with pool.Fori(0, ET - 1) as i:
                        tiles(i, True)
                    tiles(ET - 1, False)
                    pool.wait_ge(l_scattered, 64 * ET)

                @block.scalar
                def _(act):
                    def gates(u, i, s):
                        k = 3 * i + s
                        act.wait_ge(r_full[u], k + 1)
                        act.wait_ge(t1_ready[u], k)
                        nc.scalar.activation(r_[u][:, :], gate_bank[u][0][:, :], ACT.Sigmoid, bias=b_r).then_inc(r_ready[u], 1)
                        act.wait_ge(z_full[u], k + 1)
                        act.wait_ge(m_ready[u], k)
                        act.wait_ge(zh_ready[u], k)
                        nc.scalar.activation(z_[u][:, :], gate_bank[u][1][:, :], ACT.Sigmoid, bias=b_z).then_inc(z_ready[u], 1)
                        act.wait_ge(t1_ready[u], k + 1)
                        nc.scalar.activation(n_[u][:, :], t1_[u][:, :], ACT.Tanh, bias=b("ih_n")).then_inc(n_ready[u], 1)

                    def h_rows(u, i, s):
                        act.wait_ge(hr_stored[u], 32 * i + 16 * s)
                        act.wait_ge(misc_full[u], use(u, f"h{s + 1}", i) + 1)
                        nc.scalar.activation(hr_[u][:, :, :].rearrange("p c f -> p (c f)"), misc[u][:, :],
                                             ACT.Copy).then_inc(hr_ready[u], 1)

                    with act.Fori(0, ET) as i:
                        for u in range(STREAMS):
                            act.wait_ge(misc_full[u], use(u, "xT", i) + 1)
                            nc.scalar.activation(xT[u][:, :], misc[u][:, :], ACT.Copy).then_inc(xT_ready[u], 1)
                        act.wait_ge(misc_full[0], use(0, "dfT", i) + 1)
                        act.wait_ge(ef_ready, i)
                        nc.scalar.activation(dfT[:, :], misc[0][:, :], ACT.Copy).then_inc(dfT_ready, 1)
                        act.wait_ge(misc_full[1], use(1, "xdT", i) + 1)
                        nc.scalar.activation(xdT[:, :], misc[1][:, :], ACT.Copy).then_inc(xdT_ready, 1)
                        for u in range(STREAMS):
                            act.wait_ge(misc_full[u], use(u, "mlp", i) + 1)
                            act.wait_ge(y_ready[u], i)
                            nc.scalar.activation(relu_[u][:, :, :].rearrange("p c f -> p (c f)"), misc[u][:, :],
                                                 ACT.Relu).then_inc(relu_ready[u], 1)
                        act.wait_ge(misc_full[0], use(0, "pre", i) + 1)
                        nc.scalar.activation(erelu[:, :], misc[0][:, :], ACT.Relu, bias=b("edge")).then_inc(pre_ready, 1)
                        for u in range(STREAMS):
                            act.wait_ge(misc_full[u], use(u, "x1T", i) + 1)
                            act.wait_ge(fin_full[u], i)
                            nc.scalar.activation(x1T[u][:, :], misc[u][:, :], ACT.Copy).then_inc(x1T_ready[u], 1)
                        for u in range(STREAMS):
                            gates(u, i, 0)
                        act.wait_ge(misc_full[1], use(1, "emlp", i) + 1)
                        act.wait_ge(ey_ready, i)
                        nc.scalar.activation(emlp[:, :, :].rearrange("p c f -> p (c f)"), misc[1][:, :],
                                             ACT.Relu).then_inc(emlp_ready, 1)
                        h_rows(0, i, 0)
                        gates(0, i, 1)
                        h_rows(1, i, 0)
                        gates(1, i, 1)
                        act.wait_ge(misc_full[1], use(1, "ex1T", i) + 1)
                        act.wait_ge(ex1_stored, 32 * i)
                        nc.scalar.activation(ex1T[:, :], misc[1][:, :], ACT.Copy).then_inc(ex1T_ready, 1)
                        h_rows(0, i, 1)
                        gates(0, i, 2)
                        h_rows(1, i, 1)
                        gates(1, i, 2)
                        for u in range(STREAMS):
                            act.wait_ge(fin_full[u], i + 1)
                            act.wait_ge(fin_ready[u], i)
                            nc.scalar.activation(gate_[u][:, :, :].rearrange("p c f -> p (c f)"), gate_bank[u][0][:, :],
                                                 ACT.Sigmoid).then_inc(gate_ready[u], 1)

                @block.vector
                def _(v):
                    def norm(y_t, st, mv, ve, rs, o, seq, k, ve_done, rs_done, ready, free):
                        for c in range(CH):
                            ins = nc.vector.bn_stats(st[:, c, :], y_t[:, c, :])
                        ins.then_inc(seq, 1)
                        v.wait_ge(seq, 2 * k + 1)
                        v.sem_inc(v_passed, 1)
                        for c in range(CH):
                            ins = nc.vector.bn_aggr(mv[:, c, :], st[:, c, :])
                        ins.then_inc(seq, 1)
                        v.wait_ge(seq, 2 * k + 2)
                        nc.vector.tensor_scalar(ve[:, :], mv[:, :, 1], LN_EPS, None, ALU.add).then_inc(ve_done, 1)
                        for s_, v_ in free:
                            v.wait_ge(s_, v_)
                        v.wait_ge(rs_done, k + 1)
                        for c in range(CH):
                            ins = nc.vector.tensor_scalar(o[:, c, :], y_t[:, c, :], mv[:, c, 0:1], rs[:, c:c + 1],
                                                          ALU.subtract, ALU.mult)
                        ins.then_inc(ready, 1)

                    def step(u, i, s):
                        k = 3 * i + s
                        v.wait_ge(hn_full[u], k + 1)
                        v.wait_ge(r_ready[u], k + 1)
                        v.wait_ge(n_ready[u], k)
                        nc.vector.scalar_tensor_tensor(t1_[u][:, :], gate_bank[u][2][:, :], b("hh_n"), r_[u][:, :],
                                                       ALU.add, ALU.mult).then_inc(t1_ready[u], 1)
                        v.wait_ge(n_ready[u], k + 1)
                        v.wait_ge(z_ready[u], k + 1)
                        nc.vector.scalar_tensor_tensor(m_[u][:, :], z_[u][:, :], 1.0, n_[u][:, :],
                                                       ALU.subtract, ALU.mult).then_inc(m_ready[u], 1)
                        v.wait_ge(m_ready[u], k + 1)
                        v.wait_ge(zh_ready[u], k + 1)
                        if s == 0:
                            v.wait_ge(fin_full[u], i)
                        nc.vector.tensor_tensor(h_[u][:, :], zh_[u][:, :], m_[u][:, :], ALU.subtract).then_inc(h_ready[u], 1)

                    nc.vector.memset(carry[:, :], 0.0).then_inc(carry_ready, 1)
                    with v.Fori(0, ET) as i:
                        v.wait_ge(e_gathered, 128 * i + 128)
                        nc.vector.tensor_tensor(df[:, :, :], xd[:, :, :], xs[:, :, :], ALU.subtract).then_inc(df_ready, 1)
                        for u in range(STREAMS):
                            v.wait_ge(relu_ready[u], i + 1)
                            nc.vector.scalar_tensor_tensor(y[u][:, :, :], xr[u][:, :, :], 2.0, relu_[u][:, :, :],
                                                           ALU.mult, ALU.add).then_inc(y_ready[u], 1)
                            v.wait_ge(y_ready[u], i + 1)
                            norm(y[u], st_[u], mv_[u], ve_[u], rs_[u], x1r[u], st_ready[u], 2 * i, ve_ready[u],
                                 rs_ready[u], x1_ready[u], [(x1_stored[u], 16 * i)])
                        v.wait_ge(pre_ready, i + 1)
                        nc.vector.tensor_tensor(ef[:, :], erelu[:, :], dfT[:, :], ALU.add).then_inc(ef_ready, 1)
                        v.wait_ge(ef_ready, i + 1)
                        v.wait_ge(carry_ready, i + 1)
                        v.wait_ge(e_aux, 32 * i + 32)
                        v.wait_ge(emlp_ready, i)
                        nc.vector.tensor_tensor_scan(emax[:, :], restart[:, :], ef[:, :], carry[:, :],
                                                     ALU.add, ALU.max).then_inc(emax_ready, 1)
                        v.wait_ge(emax_ready, i + 1)
                        nc.vector.tensor_copy(carry[:, :], emax[:, TILE - 1:TILE]).then_inc(carry_ready, 1)
                        for u in range(STREAMS):
                            step(u, i, 0)
                        v.wait_ge(emlp_ready, i + 1)
                        nc.vector.scalar_tensor_tensor(ey[:, :, :], xd[:, :, :], 2.0, emlp[:, :, :],
                                                       ALU.mult, ALU.add).then_inc(ey_ready, 1)
                        v.wait_ge(ey_ready, i + 1)
                        norm(ey, est, emv, eve, ers, ex1r, e_stat, i, ve_e, rs_e, ex1_ready, [(ex1_stored, 32 * i)])
                        for s in range(1, STEPS):
                            for u in range(STREAMS):
                                step(u, i, s)
                        for u in range(STREAMS):
                            v.wait_ge(gate_ready[u], i + 1)
                            nc.vector.tensor_tensor(fin_[u][:, :, :].rearrange("p c f -> p (c f)"),
                                                    gate_bank[u][1][:, :],
                                                    gate_[u][:, :, :].rearrange("p c f -> p (c f)"),
                                                    ALU.mult).then_inc(fin_ready[u], 1)
                            v.wait_ge(fin_ready[u], i + 1)
                            nc.vector.tensor_tensor(yo_[u][:, :, :], fin_[u][:, :, :], x1r[u][:, :, :],
                                                    ALU.add).then_inc(yo_ready[u], 1)
                            v.wait_ge(yo_ready[u], i + 1)
                            norm(yo_[u], st_[u], mv_[u], ve_[u], rs_[u], or_[u], st_ready[u], 2 * i + 1, ve_ready[u],
                                 rs_ready[u], out_ready[u], [(out_stored[u], 16 * i)])

                @block.tensor
                def _(pe):
                    def gates(u, i, s):
                        k = 3 * i + s
                        h = x1T[u] if s == 0 else h_[u]
                        if s == 0:
                            pe.wait_ge(x1T_ready[u], i + 1)
                            pe.wait_ge(gate_ready[u], i)
                            pe.wait_ge(fin_ready[u], i)
                        else:
                            pe.wait_ge(h_ready[u], k)
                        bank = gate_bank[u]
                        product(bank[0][:, :], "hh_r", h[:, :], True, True).then_inc(r_full[u], 1)
                        product(bank[2][:, :], "hh_n", h[:, :], True, True).then_inc(hn_full[u], 1)
                        product(bank[1][:, :], "hh_z", h[:, :], True, True).then_inc(z_full[u], 1)

                    def h_rows(u, i, s):
                        if s == 0:
                            pe.wait_ge((x1T_ready[0], emlp_ready)[u], i + 1)
                        elif u == 0:
                            pe.wait_ge(hr_ready[0], 2 * i + 1)
                        else:
                            pe.wait_ge(ex1T_ready, i + 1)
                        pe.wait_ge(h_ready[u], 3 * i + s + 1)
                        flip(misc[u], chunks(h_[u][:, :])).then_inc(misc_full[u], 1)

                    with pe.Fori(0, ET) as i:
                        for u in range(STREAMS):
                            pe.wait_ge(x_loaded[u], 16 * i + 16)
                            pe.wait_ge(hr_ready[u], 2 * i)
                            flip(misc[u], xr[u]).then_inc(misc_full[u], 1)
                        pe.wait_ge(df_ready, i + 1)
                        pe.wait_ge(xT_ready[0], i + 1)
                        flip(misc[0], df).then_inc(misc_full[0], 1)
                        pe.wait_ge(e_gathered, 128 * i + 128)
                        pe.wait_ge(xT_ready[1], i + 1)
                        flip(misc[1], xd).then_inc(misc_full[1], 1)
                        for u in range(STREAMS):
                            pe.wait_ge(xT_ready[u], i + 1)
                            pe.wait_ge((dfT_ready, xdT_ready)[u], i + 1)
                            row_product(misc[u], [(xT[u], "mlp_x")], "mlp").then_inc(misc_full[u], 1)
                        pe.wait_ge(dfT_ready, i + 1)
                        pe.wait_ge(e_aux, 32 * i + 32)
                        pe.wait_ge(relu_ready[0], i + 1)
                        product(misc[0][:, :], "edge_x", dfT[:, :], True, False)
                        product(misc[0][:, :], "edge_f", efT[:, :], False, True, rows=F_E).then_inc(misc_full[0], 1)
                        for u in range(STREAMS):
                            pe.wait_ge(x1_ready[u], i + 1)
                            pe.wait_ge((pre_ready, relu_ready[1])[u], i + 1)
                            flip(misc[u], x1r[u]).then_inc(misc_full[u], 1)
                        for u in range(STREAMS):
                            gates(u, i, 0)
                        pe.wait_ge(xdT_ready, i + 1)
                        pe.wait_ge(emax_ready, i + 1)
                        pe.wait_ge(x1T_ready[1], i + 1)
                        row_product(misc[1], [(xdT, "mlp_x"), (emax, "mlp_m")], "mlp").then_inc(misc_full[1], 1)
                        h_rows(0, i, 0)
                        gates(0, i, 1)
                        h_rows(1, i, 0)
                        gates(1, i, 1)
                        pe.wait_ge(ex1_ready, i + 1)
                        pe.wait_ge(hr_ready[1], 2 * i + 1)
                        flip(misc[1], ex1r).then_inc(misc_full[1], 1)
                        h_rows(0, i, 1)
                        gates(0, i, 2)
                        h_rows(1, i, 1)
                        gates(1, i, 2)
                        for u in range(STREAMS):
                            pe.wait_ge(h_ready[u], 3 * i + STEPS)
                            row_product(gate_bank[u][0], [(h_[u], "i_h"), (x1T[u], "i_x")], "i")
                            row_product(gate_bank[u][1], [(h_[u], "j")], "j").then_inc(fin_full[u], 1)

        with ExitStack() as own:
            def sbo(name, shape, dt=F32):
                return own.enter_context(nc.sbuf_tensor(name, shape, dt))

            rows = [P, CH, P]
            cols = [P, TILE]
            idx, at, seg = sbo("idx", [P, CH], I32), sbo("at", [P, CH], I32), sbo("seg", [P, CH], I32)
            g, gT, msg, a = sbo("g", rows), sbo("gT", cols), sbo("msg", cols), sbo("a", cols)
            acarry = sbo("acarry", [P, 1])
            same, mask = sbo("same", cols, BF16), sbo("mask", [P, KT - 1, TILE], U8)
            h, r_, z_, n_, t1_, t2_, zh_, m_, hn_ = (sbo(n, cols) for n in (
                "h", "er_", "ez_", "en_", "et1_", "et2_", "ezh_", "em_", "ehn_"))
            hrow, x1r, x1T, gate_, fin_, yo_, or_ = (sbo(n, s_) for n, s_ in (
                ("hrow", rows), ("fx1r", rows), ("fx1T", cols), ("fgate", rows), ("ffin", rows), ("fyo", rows), ("for_", rows)))
            st_, mv_, ve_, rs_ = sbo("fst", [P, CH, 6]), sbo("fmv", [P, CH, 2]), sbo("fve", [P, CH]), sbo("frs", [P, CH])
            gT_bank, t_bank, row_bank = banks[0], [banks[1], banks[2]], banks[3]
            r_bank, z_bank, hn_bank, in_bank = banks[4:8]

            (idx_loaded, at_gathered, at_stored, gathered, same_loaded, mask_loaded, gT_full, gT_ready, t_full,
             msg_ready, a_ready, acarry_ready, h_loaded, r_full, hn_full, in_full, z_full, r_ready, z_ready, n_ready,
             t1_ready, t2_ready, zh_ready, m_ready, hn_ready, row_full, hrow_ready, h_stored) = (sem(f"a_{n}") for n in (
                 "idx_loaded at_gathered at_stored gathered same_loaded mask_loaded gT_full gT_ready t_full "
                 "msg_ready a_ready acarry_ready h_loaded r_full hn_full in_full z_full r_ready z_ready n_ready "
                 "t1_ready t2_ready zh_ready m_ready hn_ready row_full hrow_ready h_stored").split())
            (x1_loaded, x1T_loaded, seg_loaded, gate_full, j_full, gate_ready, fin_ready, yo_ready, f_stat, ve_ready,
             rs_ready, f_ready, f_scattered) = (sem(f"f_{n}") for n in (
                 "x1_loaded x1T_loaded seg_loaded gate_full j_full gate_ready fin_ready yo_ready f_stat ve_ready "
                 "rs_ready f_ready f_scattered").split())

            def tile_of(t, i):
                return t[bass.ds(i, 1), :, :].rearrange("t p c -> (t p) c")

            def pipeline(eng, s, before, body):
                before()
                body(0, None)
                with eng.Fori(1, ET) as i:
                    body(i, i - 1)
                body(None, ET - 1)

            for s in range(STEPS):
                n = s * ET
                final = s == STEPS - 1
                with nc.Block() as block:
                    @block.sync
                    def _(sp):
                        def body(i, j):
                            if i is not None:
                                sp.wait_ge(gathered, 64 * (n + i))
                                if s == 0:
                                    sp.dma_start(idx[:, :], tile_of(src_t, i)).then_inc(idx_loaded, 16)
                                else:
                                    sp.dma_start(at[:, :], tile_of(src_rows, i)).then_inc(idx_loaded, 16)
                                sp.wait_ge(a_ready, n + i)
                                sp.dma_start(mask[:, :, :], mask_d[:, bass.ds(i * TILE, TILE)].unsqueeze(0)
                                             .to_broadcast([P, KT - 1, TILE])).then_inc(mask_loaded, 16)
                                sp.dma_start(same[:, :], same_d[:, bass.ds(i * TILE, TILE)]
                                             .to_broadcast([P, TILE])).then_inc(same_loaded, 16)
                            if j is not None:
                                sp.wait_ge(hn_ready, n + j)
                                sp.dma_start(h[:, :], tile_of(states[s], j)).then_inc(h_loaded, 16)
                                if final:
                                    sp.wait_ge(f_ready, j)
                                    sp.dma_start(x1r[:, :, :], edge_rows(tables[0], j)).then_inc(x1_loaded, 16)
                                    sp.dma_start(x1T[:, :], tile_of(states[0], j)).then_inc(x1T_loaded, 16)
                                    sp.wait_ge(f_scattered, 64 * j)
                                    sp.sem_inc(sp_passed, 1)
                                    sp.dma_start(seg[:, :], tile_of(last_t, j)).then_inc(seg_loaded, 16)
                                else:
                                    sp.wait_ge(hrow_ready, n + j + 1)
                                    sp.dma_start(edge_rows(tables[s + 1], j), hrow[:, :, :]).then_inc(h_stored, 16)
                                    sp.dma_start(tile_of(states[s + 1], j), hn_[:, :]).then_inc(h_stored, 16)
                            if i is not None and s == 0:
                                sp.wait_ge(at_gathered, 64 * (i + 1))
                                sp.dma_start(tile_of(src_rows, i), at[:, :]).then_inc(at_stored, 16)

                        pipeline(sp, s, lambda: None, body)
                        if final:
                            pass
                        else:
                            sp.wait_ge(h_stored, 32 * (n + ET))
                        if s == 0:
                            sp.wait_ge(at_stored, 16 * ET)

                    @block.gpsimd
                    def _(pool):
                        def body(i, j):
                            if i is not None:
                                if s == 0:
                                    pool.wait_ge(at_stored, 16 * i)
                                    pool.wait_ge(gathered, 64 * i)
                                    pool.wait_ge(idx_loaded, 16 * (i + 1))
                                    pool.sem_inc(passed, 1)
                                    for c in range(CH):
                                        nc.gpsimd.indirect_dma_start(
                                            out=at[:, c:c + 1], out_offset=None, in_=where[:, :],
                                            in_offset=bass.IndirectOffsetOnAxis(ap=idx[:, c:c + 1], axis=0),
                                            bounds_check=NPAD - 1, oob_is_err=False).then_inc(at_gathered, 16)
                                    pool.wait_ge(at_gathered, 64 * (i + 1))
                                else:
                                    pool.wait_ge(idx_loaded, 16 * (n + i + 1))
                                pool.wait_ge(gT_full, n + i)
                                pool.sem_inc(passed, 1)
                                for c in range(CH):
                                    nc.gpsimd.indirect_dma_start(
                                        out=g[:, c, :], out_offset=None, in_=tables[s][:, :],
                                        in_offset=bass.IndirectOffsetOnAxis(ap=at[:, c:c + 1], axis=0),
                                        bounds_check=NPAD + EPAD - 1, oob_is_err=False).then_inc(gathered, 16)
                            if j is not None:
                                pool.wait_ge(h_loaded, 16 * (n + j + 1))
                                pool.wait_ge(z_ready, n + j + 1)
                                nc.gpsimd.tensor_tensor(zh_[:, :], z_[:, :], h[:, :], ALU.mult).then_inc(zh_ready, 1)
                                if final:
                                    pool.wait_ge(ve_ready, j + 1)
                                    nc.gpsimd.tensor_tensor(rs_[:, :], ve_[:, :], half[:, :], ALU.pow).then_inc(rs_ready, 1)
                                    pool.wait_ge(f_ready, j + 1)
                                    pool.wait_ge(seg_loaded, 16 * (j + 1))
                                    pool.sem_inc(passed, 1)
                                    for c in range(CH):
                                        nc.gpsimd.indirect_dma_start(
                                            out=out[:, :], out_offset=bass.IndirectOffsetOnAxis(ap=seg[:, c:c + 1], axis=0),
                                            in_=or_[:, c, :], in_offset=None,
                                            bounds_check=NPAD - 1, oob_is_err=False).then_inc(f_scattered, 16)

                        pipeline(pool, s, lambda: None, body)
                        if final:
                            pool.wait_ge(f_scattered, 64 * ET)

                    @block.scalar
                    def _(act):
                        def body(i, j):
                            if i is not None:
                                act.wait_ge(gT_full, n + i + 1)
                                act.wait_ge(t_full, KT * (n + i))
                                nc.scalar.activation(gT[:, :], gT_bank[:, :], ACT.Copy).then_inc(gT_ready, 1)
                            if j is not None:
                                act.wait_ge(r_full, n + j + 1)
                                act.wait_ge(t1_ready, n + j)
                                nc.scalar.activation(r_[:, :], r_bank[:, :], ACT.Sigmoid, bias=b_r).then_inc(r_ready, 1)
                                act.wait_ge(t2_ready, n + j + 1)
                                act.wait_ge(m_ready, n + j)
                                nc.scalar.activation(n_[:, :], t2_[:, :], ACT.Tanh, bias=b("ih_n")).then_inc(n_ready, 1)
                                act.wait_ge(z_full, n + j + 1)
                                act.wait_ge(zh_ready, n + j)
                                nc.scalar.activation(z_[:, :], z_bank[:, :], ACT.Sigmoid, bias=b_z).then_inc(z_ready, 1)
                            if i is not None:
                                act.wait_ge(t_full, KT * (n + i) + 1)
                                act.wait_ge(a_ready, n + i)
                                nc.scalar.activation(msg[:, :], t_bank[0][:, :], ACT.Identity, bias=b("et0")).then_inc(msg_ready, 1)
                            if j is not None:
                                if final:
                                    act.wait_ge(gate_full, j + 1)
                                    act.wait_ge(fin_ready, j)
                                    nc.scalar.activation(gate_[:, :, :].rearrange("p c f -> p (c f)"), row_bank[:, :],
                                                         ACT.Sigmoid).then_inc(gate_ready, 1)
                                else:
                                    act.wait_ge(row_full, n + j + 1)
                                    act.wait_ge(h_stored, 32 * (n + j))
                                    nc.scalar.activation(hrow[:, :, :].rearrange("p c f -> p (c f)"), row_bank[:, :],
                                                         ACT.Copy).then_inc(hrow_ready, 1)

                        pipeline(act, s, lambda: None, body)

                    @block.vector
                    def _(v):
                        def before():
                            nc.vector.memset(acarry[:, :], 0.0).then_inc(acarry_ready, 1)

                        def body(i, j):
                            if j is not None:
                                v.wait_ge(hn_full, n + j + 1)
                                v.wait_ge(r_ready, n + j + 1)
                                nc.vector.scalar_tensor_tensor(t1_[:, :], hn_bank[:, :], b("hh_n"), r_[:, :],
                                                               ALU.add, ALU.mult).then_inc(t1_ready, 1)
                                v.wait_ge(in_full, n + j + 1)
                                v.wait_ge(t1_ready, n + j + 1)
                                v.wait_ge(n_ready, n + j)
                                nc.vector.tensor_tensor(t2_[:, :], in_bank[:, :], t1_[:, :], ALU.add).then_inc(t2_ready, 1)
                                v.wait_ge(n_ready, n + j + 1)
                                v.wait_ge(z_ready, n + j + 1)
                                nc.vector.scalar_tensor_tensor(m_[:, :], z_[:, :], 1.0, n_[:, :],
                                                               ALU.subtract, ALU.mult).then_inc(m_ready, 1)
                                v.wait_ge(m_ready, n + j + 1)
                                v.wait_ge(zh_ready, n + j + 1)
                                if final:
                                    v.wait_ge(j_full, j)
                                else:
                                    v.wait_ge(h_stored, 32 * (n + j))
                                nc.vector.tensor_tensor(hn_[:, :], zh_[:, :], m_[:, :], ALU.subtract).then_inc(hn_ready, 1)
                            if i is not None:
                                v.wait_ge(mask_loaded, 16 * (n + i + 1))
                                for k in range(1, KT):
                                    v.wait_ge(msg_ready, KT * (n + i) + k)
                                    v.wait_ge(t_full, KT * (n + i) + k + 1)
                                    v.sem_inc(v_passed, 1)
                                    nc.vector.copy_predicated(msg[:, :], mask[:, k - 1, :], t_bank[k % 2][:, :]).then_inc(msg_ready, 1)
                                v.wait_ge(msg_ready, KT * (n + i) + KT)
                                v.wait_ge(same_loaded, 16 * (n + i + 1))
                                v.wait_ge(acarry_ready, n + s + i + 1)
                                v.wait_ge(z_full, n + i)
                                nc.vector.tensor_tensor_scan(a[:, :], same[:, :], msg[:, :], acarry[:, :],
                                                             ALU.mult, ALU.add).then_inc(a_ready, 1)
                                v.wait_ge(a_ready, n + i + 1)
                                nc.vector.tensor_copy(acarry[:, :], a[:, TILE - 1:TILE]).then_inc(acarry_ready, 1)
                            if j is not None and final:
                                v.wait_ge(gate_ready, j + 1)
                                v.wait_ge(j_full, j + 1)
                                flat = "p c f -> p (c f)"
                                nc.vector.tensor_tensor(fin_[:, :, :].rearrange(flat), r_bank[:, :],
                                                        gate_[:, :, :].rearrange(flat), ALU.mult).then_inc(fin_ready, 1)
                                v.wait_ge(fin_ready, j + 1)
                                v.wait_ge(x1_loaded, 16 * (j + 1))
                                nc.vector.tensor_tensor(yo_[:, :, :], fin_[:, :, :], x1r[:, :, :], ALU.add).then_inc(yo_ready, 1)
                                v.wait_ge(yo_ready, j + 1)
                                for c in range(CH):
                                    ins = nc.vector.bn_stats(st_[:, c, :], yo_[:, c, :])
                                ins.then_inc(f_stat, 1)
                                v.wait_ge(f_stat, 2 * j + 1)
                                v.sem_inc(v_passed, 1)
                                for c in range(CH):
                                    ins = nc.vector.bn_aggr(mv_[:, c, :], st_[:, c, :])
                                ins.then_inc(f_stat, 1)
                                v.wait_ge(f_stat, 2 * j + 2)
                                nc.vector.tensor_scalar(ve_[:, :], mv_[:, :, 1], LN_EPS, None, ALU.add).then_inc(ve_ready, 1)
                                v.wait_ge(f_scattered, 64 * j)
                                v.wait_ge(rs_ready, j + 1)
                                for c in range(CH):
                                    ins = nc.vector.tensor_scalar(or_[:, c, :], yo_[:, c, :], mv_[:, c, 0:1], rs_[:, c:c + 1],
                                                                  ALU.subtract, ALU.mult)
                                ins.then_inc(f_ready, 1)

                        pipeline(v, s, before, body)

                    @block.tensor
                    def _(pe):
                        def body(i, j):
                            if i is not None:
                                pe.wait_ge(gathered, 64 * (n + i + 1))
                                pe.wait_ge(gT_ready, n + i)
                                flip(gT_bank, g).then_inc(gT_full, 1)
                            if j is not None:
                                pe.wait_ge(h_loaded, 16 * (n + j + 1))
                                pe.wait_ge(a_ready, n + j + 1)
                                if final:
                                    pe.wait_ge(fin_ready, j)
                                product(r_bank[:, :], "hh_r", h[:, :], True, False)
                                product(r_bank[:, :], "ih_r", a[:, :], False, True).then_inc(r_full, 1)
                                product(hn_bank[:, :], "hh_n", h[:, :], True, True).then_inc(hn_full, 1)
                                pe.wait_ge(t2_ready, n + j)
                                product(in_bank[:, :], "ih_n", a[:, :], True, True).then_inc(in_full, 1)
                                product(z_bank[:, :], "hh_z", h[:, :], True, False)
                                product(z_bank[:, :], "ih_z", a[:, :], False, True).then_inc(z_full, 1)
                            if i is not None:
                                pe.wait_ge(gT_ready, n + i + 1)
                                pe.wait_ge(a_ready, n + i)
                                for k in range(KT):
                                    if k >= 2:
                                        pe.wait_ge(msg_ready, KT * (n + i) + k - 1)
                                    mm = product(t_bank[k % 2][:, :], f"et{k}", gT[:, :], True, k == 0)
                                    if k:
                                        mm = bias_cols(t_bank[k % 2][:, :], f"et{k}")
                                    mm.then_inc(t_full, 1)
                            if j is not None:
                                pe.wait_ge(hn_ready, n + j + 1)
                                if final:
                                    pe.wait_ge(x1T_loaded, 16 * (j + 1))
                                    pe.wait_ge(gate_ready, j)
                                    row_product(row_bank, [(hn_, "i_h"), (x1T, "i_x")], "i").then_inc(gate_full, 1)
                                    row_product(r_bank, [(hn_, "j")], "j").then_inc(j_full, 1)
                                else:
                                    pe.wait_ge(hrow_ready, n + j)
                                    flip(row_bank, chunks(hn_[:, :])).then_inc(row_full, 1)

                        pipeline(pe, s, lambda: None, body)


def kernel(**inputs):
    import numpy as np
    import concourse.bacc as bacc
    from concourse.bass_utils import run_bass_kernel_spmd

    q = {k: np.asarray(v) for k, v in inputs.items()}
    x = np.zeros((NPAD, P), np.float32)
    x[:N] = q["x"]
    dst = np.full(EPAD + 2, N, np.int32)
    dst[0] = -1
    dst[1:E + 1] = q["dst"]
    src = np.full(EPAD, N, np.int32)
    src[:E] = q["src"]
    kind = np.zeros(EPAD, np.int32)
    kind[:E] = q["edge_type_4"]
    ef = np.zeros((EPAD, F_E), np.float32)
    ef[:E] = q["edge_attr_64"]

    def by_chunk(a):
        return np.ascontiguousarray(a.reshape(ET, CH, P).transpose(0, 2, 1))

    def linear(a):
        return np.ascontiguousarray(a.reshape(P, ECOL))

    we = np.zeros((2 * P, P), np.float32)
    we[:P + F_E] = q["L0_gnn_W_edge"]
    wm, iw = q["L0_gnn_W_mlp"], q["L1_gnn_i_w"].T
    parts = [we[:P], we[P:], wm[:P], wm[P:]] + [q["L1_gnn_W_et"][k].T for k in range(KT)]
    parts += [q["L1_gnn_W_ih"][k * P:(k + 1) * P].T for k in range(3)]
    parts += [q["L1_gnn_W_hh"][k * P:(k + 1) * P].T for k in range(3)]
    parts += [iw[:P], iw[P:], q["L1_gnn_j_w"].T]
    cols = [q["L0_gnn_b_edge"]] + [q["L1_gnn_b_et"][k] for k in range(KT)]
    cols += [q["L1_gnn_b_ih"][k * P:(k + 1) * P] for k in range(3)]
    cols += [q["L1_gnn_b_hh"][k * P:(k + 1) * P] for k in range(3)]
    brows = [q["L0_gnn_b_mlp"], q["L1_gnn_i_b"], q["L1_gnn_j_b"]] + [q["L1_gnn_b_et"][k] for k in range(KT)]
    arrays = {
        "x_rows": x,
        "dst_lin": linear(dst[1:-1]), "prev_lin": linear(dst[:-2]), "type_lin": linear(kind),
        "dst_t": by_chunk(dst[1:-1]), "next_t": by_chunk(dst[2:]), "src_t": by_chunk(src),
        "ef_t": np.ascontiguousarray(ef.T),
        "weights": np.ascontiguousarray(np.concatenate(parts, axis=1)),
        "biases": np.ascontiguousarray(np.stack(cols, axis=1)),
        "bias_rows": np.ascontiguousarray(np.concatenate(brows).reshape(1, -1)),
    }
    nc = bacc.Bacc("TRN2", target_bir_lowering=False, num_devices=1)
    args = [nc.dram_tensor(k, a.shape, mybir.dt.from_np(a.dtype), kind="ExternalInput").ap() for k, a in arrays.items()]
    out = nc.dram_tensor("out_rows", (NPAD, P), F32, kind="ExternalOutput").ap()
    build(nc, *args, out)
    r = run_bass_kernel_spmd(nc, [arrays], core_ids=[0])
    return r.results[0]["out_rows"][:N]
```

```python
from contextlib import ExitStack

import concourse.bass as bass
from concourse import mybir

P = 128
N = 50000
E = 25000
CH = 4
TILE = P * CH
ET = -(-E // TILE)
EPAD = ET * TILE
NT = -(-N // TILE)
NPAD = NT * TILE
ECOL = EPAD // P
KT = 4
F_E = 64
STEPS = 3
STREAMS = 2
NOWHERE = 1 << 20
LN_EPS = 1e-5
RESTART = -3.0e38
assert NT == STREAMS * ET

ALU = mybir.AluOpType
ACT = mybir.ActivationFunctionType
F32 = mybir.dt.float32
BF16 = mybir.dt.bfloat16
F32R = mybir.dt.float32r
I32 = mybir.dt.int32
U8 = mybir.dt.uint8

W_NAMES = (["edge_x", "edge_f", "mlp_x", "mlp_m"] + [f"et{k}" for k in range(KT)]
           + ["ih_r", "ih_z", "ih_n", "hh_r", "hh_z", "hh_n", "i_h", "i_x", "j"])
W3_NAMES = [f"et{k}" for k in range(KT)] + ["ih_r", "ih_z", "ih_n", "hh_r", "hh_z", "hh_n"]
W3_FROM = W_NAMES.index(W3_NAMES[0])
assert W_NAMES[W3_FROM:W3_FROM + len(W3_NAMES)] == W3_NAMES
PARTS = 3
B_NAMES = ["edge"] + [f"et{k}" for k in range(KT)] + ["ih_r", "ih_z", "ih_n", "hh_r", "hh_z", "hh_n"]
R_NAMES = ["mlp", "i", "j"] + [f"et{k}" for k in range(KT)]


def freed(eng, semaphore, value):
    if not (isinstance(value, int) and value <= 0):
        eng.wait_ge(semaphore, value)


def build(nc, x, dst_lin, prev_lin, type_lin, dst_t, next_t, src_t, ef_t, weights, biases, bias_rows, out):
    with ExitStack() as ctx:
        def sb(name, shape, dt=F32):
            return ctx.enter_context(nc.sbuf_tensor(name, shape, dt))

        def sem(name):
            return ctx.enter_context(nc.semaphore(name))

        def sems(name, n=STREAMS):
            return [sem(f"{name}{k}") for k in range(n)]

        def dram(name, shape, dt=F32):
            return nc.dram_tensor(name, shape, dt, kind="Internal").ap()

        tables = [dram(f"table{s}", (NPAD + EPAD, P)) for s in range(STEPS)]
        states = [dram(f"state{s}", (ET, P, TILE)) for s in range(STEPS)]
        where = dram("where", (NPAD, 1), I32)
        src_rows = dram("src_rows", (ET, P, CH), I32)
        last_t = dram("last_t", (ET, P, CH), I32)
        rows_t = dram("rows_t", (ET, P, CH), I32)
        same_d = dram("same_d", (1, EPAD), BF16)
        restart_d = dram("restart_d", (1, EPAD), BF16)
        mask_d = dram("mask_d", (KT - 1, EPAD), U8)

        wt = sb("wt", [P, len(W_NAMES) * P])
        bs = sb("bs", [P, len(B_NAMES)])
        brz = sb("brz", [P, 2])
        bpart = sb("bpart", [PARTS, len(R_NAMES) * P], BF16)
        ones = sb("ones", [PARTS, TILE], BF16)
        w_hi, w_lo = (sb(n, [P, len(W3_NAMES) * P], F32R) for n in ("w_hi", "w_lo"))
        ident = sb("ident", [P, P])
        half = sb("half", [P, CH])

        def w(name, rows=P):
            k = W_NAMES.index(name)
            return wt[0:rows, k * P:(k + 1) * P]

        def b(name):
            k = B_NAMES.index(name)
            return bs[:, k:k + 1]

        b_r, b_z = brz[:, 0:1], brz[:, 1:2]

        passed, v_passed, sp_passed = sem("passed"), sem("v_passed"), sem("sp_passed")

        banks = [ctx.enter_context(nc.psum_tensor(f"bank{k}", [P, TILE], F32)) for k in range(8)]

        def product(o, name, operand, first, last, rows=P):
            return nc.tensor.matmul(o, w(name, rows), operand, start=first, stop=last)

        def product3(bank, name, hi, lo, first, last):
            k = W3_NAMES.index(name) * P
            nc.tensor.matmul(bank[:, :], w_hi[:, k:k + P], hi[:, :], start=first, stop=False)
            nc.tensor.matmul(bank[:, :], w_hi[:, k:k + P], lo[:, :], start=False, stop=False)
            return nc.tensor.matmul(bank[:, :], w_lo[:, k:k + P], hi[:, :], start=False, stop=last)

        def bias_rows_into(o, name):
            k = R_NAMES.index(name) * P
            return nc.tensor.matmul(o, ones[:, 0:P], bpart[:, k:k + P], start=False, stop=True)

        def bias_cols(o, name):
            k = R_NAMES.index(name) * P
            return nc.tensor.matmul(o, bpart[:, k:k + P], ones[:, :], start=False, stop=True)

        def flip(o, rows):
            for c in range(CH):
                mm = nc.tensor.transpose(o[:, c * P:(c + 1) * P], rows[:, c, :], ident[:, :])
            return mm

        def chunks(t):
            return t.rearrange("p (c f) -> p c f", c=CH)

        def row_product(bank, terms, bias):
            for c in range(CH):
                o = bank[:, c * P:(c + 1) * P]
                for n, (operand, name) in enumerate(terms):
                    nc.tensor.matmul(o, operand[:, c * P:(c + 1) * P], w(name), start=n == 0, stop=False)
                mm = bias_rows_into(o, bias)
            return mm

        with ExitStack() as own:
            def sbo(name, shape, dt=I32):
                return own.enter_context(nc.sbuf_tensor(name, shape, dt))

            dl, pl, tl = sbo("dl", [P, ECOL]), sbo("pl", [P, ECOL]), sbo("tl", [P, ECOL])
            dt_, nt_ = sbo("dt_", [P, ECOL]), sbo("nt_", [P, ECOL])
            same_s, restart_s = sbo("same_s", [P, ECOL], BF16), sbo("restart_s", [P, ECOL], BF16)
            mask_s = sbo("mask_s", [P, KT - 1, ECOL], U8)
            more = sbo("more", [P, ECOL])
            last_s, rows_s, where_s = sbo("last_s", [P, ECOL]), sbo("rows_s", [P, ECOL]), sbo("where_s", [P, NPAD // P])
            brow, bres, bsum = (sbo(n, [PARTS, len(R_NAMES) * P], F32) for n in ("brow", "bres", "bsum"))
            bcut = sbo("bcut", [PARTS, len(R_NAMES) * P], BF16)
            loaded, ident_zero, pool_ready = sem("loaded"), sem("ident_zero"), sem("pool_ready")
            part, flags_ready = sem("part"), sem("flags_ready")
            setup_stored = sem("setup_stored")

            with nc.Block() as block:
                @block.sync
                def _(sp):
                    sp.dma_start(wt[:, :], weights).then_inc(loaded, 16)
                    sp.dma_start(bs[:, :], biases).then_inc(loaded, 16)
                    sp.dma_start(brow[:, :], bias_rows.to_broadcast([PARTS, len(R_NAMES) * P])).then_inc(loaded, 16)
                    for t, d in ((dl, dst_lin), (pl, prev_lin), (tl, type_lin)):
                        sp.dma_start(t[:, :], d).then_inc(loaded, 16)
                    for t, d in ((dt_, dst_t), (nt_, next_t)):
                        sp.dma_start(t[:, :].rearrange("p (t c) -> p t c", c=CH),
                                     d.rearrange("t p c -> p t c")).then_inc(loaded, 16)
                    sp.wait_ge(pool_ready, 4)
                    sp.dma_start(where.rearrange("(p c) o -> p (c o)", p=P), where_s[:, :]).then_inc(setup_stored, 16)
                    sp.dma_start(rows_t.rearrange("t p c -> p t c"),
                                 rows_s[:, :].rearrange("p (t c) -> p t c", c=CH)).then_inc(setup_stored, 16)
                    sp.wait_ge(flags_ready, 1)
                    sp.dma_start(last_t.rearrange("t p c -> p t c"),
                                 last_s[:, :].rearrange("p (t c) -> p t c", c=CH)).then_inc(setup_stored, 16)
                    sp.dma_start(same_d.rearrange("o (p c) -> (o p) c", p=P), same_s[:, :]).then_inc(setup_stored, 16)
                    sp.dma_start(restart_d.rearrange("o (p c) -> (o p) c", p=P), restart_s[:, :]).then_inc(setup_stored, 16)
                    sp.dma_start(mask_d.rearrange("k (p c) -> p k c", p=P), mask_s[:, :, :]).then_inc(setup_stored, 16)
                    sp.wait_ge(setup_stored, 96)

                @block.gpsimd
                def _(pool):
                    nc.gpsimd.memset(ident[:, :], 0.0).then_inc(ident_zero, 1)
                    pool.wait_ge(ident_zero, 1)
                    nc.gpsimd.affine_select(out=ident[:, :], in_=ident[:, :], compare_op=ALU.not_equal, fill=1.0,
                                            base=0, pattern=[[-1, P]], channel_multiplier=1).then_inc(pool_ready, 1)
                    nc.gpsimd.memset(half[:, :], -0.5).then_inc(pool_ready, 1)
                    nc.gpsimd.iota(where_s[:, :], pattern=[[1, NPAD // P]], base=0,
                                   channel_multiplier=NPAD // P).then_inc(pool_ready, 1)
                    nc.gpsimd.iota(rows_s[:, :], pattern=[[P, ECOL]], base=NPAD,
                                   channel_multiplier=1).then_inc(pool_ready, 1)

                @block.vector
                def _(v):
                    v.wait_ge(loaded, 128)
                    made = [0]

                    def made_by(ins):
                        made[0] += 1
                        ins.then_inc(part, 1)

                    nc.vector.memset(ones[:, :], 1.0)
                    made_by(nc.vector.tensor_tensor(brz[:, 0:1], b("ih_r"), b("hh_r"), ALU.add))
                    made_by(nc.vector.tensor_tensor(brz[:, 1:2], b("ih_z"), b("hh_z"), ALU.add))
                    v.wait_ge(pool_ready, 4)
                    for n in range(PARTS):
                        from_ = brow if n == 0 else bres
                        v.wait_ge(part, made[0])
                        made_by(nc.vector.tensor_copy(bcut[:, :], from_[:, :]))
                        v.wait_ge(part, made[0])
                        if n == 0:
                            made_by(nc.vector.tensor_scalar(bsum[:, :], bcut[:, :], ident[0:PARTS, n:n + 1], None, ALU.mult))
                        else:
                            made_by(nc.vector.scalar_tensor_tensor(bsum[:, :], bcut[:, :], ident[0:PARTS, n:n + 1], bsum[:, :],
                                                                   ALU.mult, ALU.add))
                        made_by(nc.vector.tensor_tensor(bres[:, :], from_[:, :], bcut[:, :], ALU.subtract))
                    v.wait_ge(part, made[0])
                    made_by(nc.vector.tensor_copy(bpart[:, :], bsum[:, :]))
                    split = wt[:, W3_FROM * P:(W3_FROM + len(W3_NAMES)) * P]
                    made_by(nc.vector.tensor_copy(w_hi[:, :], split))
                    v.wait_ge(part, made[0])
                    made_by(nc.vector.tensor_tensor(w_lo[:, :], split, w_hi[:, :].bitcast(F32), ALU.subtract))
                    made_by(nc.vector.tensor_tensor(same_s[:, :], dl[:, :], pl[:, :], ALU.is_equal))
                    v.wait_ge(part, made[0])
                    made_by(nc.vector.tensor_scalar(restart_s[:, :], same_s[:, :], -1.0, -RESTART, ALU.add, ALU.mult))
                    for k in range(1, KT):
                        made_by(nc.vector.tensor_scalar(mask_s[:, k - 1, :], tl[:, :], float(k), None, ALU.is_equal))
                    made_by(nc.vector.tensor_tensor(more[:, :], dt_[:, :], nt_[:, :], ALU.is_equal))
                    v.wait_ge(part, made[0])
                    nc.vector.scalar_tensor_tensor(last_s[:, :], more[:, :], float(NOWHERE), dt_[:, :],
                                                   ALU.mult, ALU.add).then_inc(flags_ready, 1)

        with ExitStack() as own:
            def sbo(name, shape, dt=F32):
                return own.enter_context(nc.sbuf_tensor(name, shape, dt))

            def pair(name, shape, dt=F32):
                return [sbo(f"{name}{u}", shape, dt) for u in range(STREAMS)]

            rows = [P, CH, P]
            cols = [P, TILE]
            xr, xT, relu_, y, x1r, x1T = (pair(n, s) for n, s in (
                ("xr", rows), ("xT", cols), ("relu_", rows), ("y", rows), ("x1r", rows), ("x1T", cols)))
            r_, z_, n_, t1_, zh_, m_, h_ = (pair(n, cols) for n in ("r_", "z_", "n_", "t1_", "zh_", "m_", "h_"))
            hr_, gate_, fin_, yo_, or_ = (pair(n, rows) for n in ("hr_", "gate_", "fin_", "yo_", "or_"))
            st_, mv_, ve_, rs_ = (pair(n, s) for n, s in (
                ("st_", [P, CH, 6]), ("mv_", [P, CH, 2]), ("ve_", [P, CH]), ("rs_", [P, CH])))
            eidx, lidx = sbo("eidx", [P, 2, CH], I32), sbo("lidx", [P, 2, CH], I32)
            xd, xs, df = sbo("xd", rows), sbo("xs", rows), sbo("df", rows)
            dfT, xdT, erelu, ef, emax = (sbo(n, cols) for n in ("dfT", "xdT", "erelu", "ef", "emax"))
            efT, restart = sbo("efT", [F_E, TILE]), sbo("restart", cols, BF16)
            carry = sbo("carry", [P, 1])
            emlp, ey, ex1r, ex1T = sbo("emlp", rows), sbo("ey", rows), sbo("ex1r", rows), sbo("ex1T", cols)
            est, emv, eve, ers = sbo("est", [P, CH, 6]), sbo("emv", [P, CH, 2]), sbo("eve", [P, CH]), sbo("ers", [P, CH])

            gate_bank = [[banks[3 * u + k] for k in range(3)] for u in range(STREAMS)]
            misc = [banks[6], banks[7]]
            USES = [["xT", "dfT", "mlp", "pre", "x1T", "h1", "h2"],
                    ["xT", "xdT", "mlp", "x1T", "emlp", "h1", "ex1T", "h2"]]
            misc_full = sems("misc_full")

            x_loaded = sems("x_loaded")
            xT_ready, relu_ready, y_ready = sems("xT_ready"), sems("relu_ready"), sems("y_ready")
            st_ready, mv_ready, ve_ready, rs_ready = sems("st_ready"), sems("mv_ready"), sems("ve_ready"), sems("rs_ready")
            x1_ready, x1T_ready, x1_stored = sems("x1_ready"), sems("x1T_ready"), sems("x1_stored")
            r_full, hn_full, z_full = sems("r_full"), sems("hn_full"), sems("z_full")
            r_ready, z_ready, n_ready = sems("r_ready"), sems("z_ready"), sems("n_ready")
            t1_ready, zh_ready, m_ready, h_ready = sems("t1_ready"), sems("zh_ready"), sems("m_ready"), sems("h_ready")
            hr_ready, hr_stored = sems("hr_ready"), sems("hr_stored")
            fin_full, gate_ready, fin_ready, yo_ready = sems("fin_full"), sems("gate_ready"), sems("fin_ready"), sems("yo_ready")
            out_ready, out_stored = sems("out_ready"), sems("out_stored")
            e_idx, e_gathered, l_idx, l_scattered = (sem(n) for n in (
                "e_idx", "e_gathered", "l_idx", "l_scattered"))
            df_ready, dfT_ready, xdT_ready, e_aux, pre_ready = (sem(n) for n in (
                "df_ready", "dfT_ready", "xdT_ready", "e_aux", "pre_ready"))
            ef_ready, emax_ready, carry_ready = (sem(n) for n in ("ef_ready", "emax_ready", "carry_ready"))
            e_stat, ve_e, rs_e = sem("e_stat"), sem("ve_e"), sem("rs_e")
            emlp_ready, ey_ready, ex1_ready, ex1T_ready, ex1_stored = (sem(n) for n in (
                "emlp_ready", "ey_ready", "ex1_ready", "ex1T_ready", "ex1_stored"))

            def use(m, name, i):
                return len(USES[m]) * i + USES[m].index(name)

            def node_rows(table, t):
                return table[bass.ds(t * TILE, TILE), :].rearrange("(p c) f -> p c f", c=CH)

            def edge_rows(table, t):
                return table[bass.ds(t * TILE + NPAD, TILE), :].rearrange("(c p) f -> p c f", p=P)

            with nc.Block() as block:
                @block.sync
                def _(sp):
                    def tile_of(a, i):
                        return a[bass.ds(i, 1), :, :].rearrange("t p c -> (t p) c")

                    def load_rows(i):
                        for u in range(STREAMS):
                            sp.wait_ge(y_ready[u], i)
                            sp.dma_start(xr[u][:, :, :], node_rows(x, i * STREAMS + u)).then_inc(x_loaded[u], 16)
                        sp.wait_ge(e_gathered, 128 * i)
                        sp.dma_start(eidx[:, 0, :], tile_of(dst_t, i)).then_inc(e_idx, 16)
                        sp.dma_start(eidx[:, 1, :], tile_of(src_t, i)).then_inc(e_idx, 16)
                        sp.wait_ge(pre_ready, i)
                        sp.dma_start(efT[:, :], ef_t[:, bass.ds(i * TILE, TILE)]).then_inc(e_aux, 16)
                        sp.wait_ge(emax_ready, i)
                        sp.sem_inc(sp_passed, 1)
                        sp.dma_start(restart[:, :], restart_d[:, bass.ds(i * TILE, TILE)].to_broadcast([P, TILE])).then_inc(e_aux, 16)

                    def load_last(i):
                        sp.wait_ge(l_scattered, 64 * i)
                        sp.dma_start(lidx[:, 0, :], tile_of(last_t, i)).then_inc(l_idx, 16)
                        sp.dma_start(lidx[:, 1, :], tile_of(rows_t, i)).then_inc(l_idx, 16)

                    def store_h(i, s, u):
                        sp.wait_ge(hr_ready[u], 2 * i + s + 1)
                        sp.dma_start(node_rows(tables[s + 1], i * STREAMS + u), hr_[u][:, :, :]).then_inc(hr_stored[u], 16)

                    def tiles(i, loads_next):
                        for u in range(STREAMS):
                            sp.wait_ge(x1_ready[u], i + 1)
                            sp.dma_start(node_rows(tables[0], i * STREAMS + u), x1r[u][:, :, :]).then_inc(x1_stored[u], 16)
                        if loads_next:
                            load_rows(i + 1)
                        store_h(i, 0, 0)
                        store_h(i, 0, 1)
                        sp.wait_ge(ex1T_ready, i + 1)
                        sp.dma_start(edge_rows(tables[0], i), ex1r[:, :, :]).then_inc(ex1_stored, 16)
                        sp.dma_start(tile_of(states[0], i), ex1T[:, :]).then_inc(ex1_stored, 16)
                        store_h(i, 1, 0)
                        store_h(i, 1, 1)
                        if loads_next:
                            load_last(i + 1)
                        for u in range(STREAMS):
                            sp.wait_ge(out_ready[u], i + 1)
                            sp.dma_start(node_rows(out, i * STREAMS + u), or_[u][:, :, :]).then_inc(out_stored[u], 16)

                    load_rows(0)
                    load_last(0)
                    with sp.Fori(0, ET - 1) as i:
                        tiles(i, True)
                    tiles(ET - 1, False)
                    for u in range(STREAMS):
                        sp.wait_ge(x1_stored[u], 16 * ET)
                        sp.wait_ge(hr_stored[u], 32 * ET)
                        sp.wait_ge(out_stored[u], 16 * ET)
                    sp.wait_ge(ex1_stored, 32 * ET)

                @block.gpsimd
                def _(pool):
                    def rstd(ve_done, value, ve, rs, ready):
                        pool.wait_ge(ve_done, value)
                        nc.gpsimd.tensor_tensor(rs[:, :], ve[:, :], half[:, :], ALU.pow).then_inc(ready, 1)

                    def keep(u, i, s):
                        pool.wait_ge(z_ready[u], 3 * i + s + 1)
                        pool.wait_ge(h_ready[u], 3 * i + s)
                        h = x1T[u] if s == 0 else h_[u]
                        nc.gpsimd.tensor_tensor(zh_[u][:, :], z_[u][:, :], h[:, :], ALU.mult).then_inc(zh_ready[u], 1)

                    def gather(i, ks):
                        pool.wait_ge(ey_ready, i)
                        pool.wait_ge(e_idx, 32 * i + 32)
                        pool.sem_inc(passed, 1)
                        for k in ks:
                            t, c = (xd, xs)[k // CH], k % CH
                            nc.gpsimd.indirect_dma_start(
                                out=t[:, c, :], out_offset=None, in_=x[:, :],
                                in_offset=bass.IndirectOffsetOnAxis(ap=eidx[:, k // CH, c:c + 1], axis=0),
                                bounds_check=NPAD - 1, oob_is_err=False).then_inc(e_gathered, 16)

                    def locate(i, c):
                        pool.wait_ge(l_idx, 32 * i + 32)
                        pool.sem_inc(passed, 1)
                        nc.gpsimd.indirect_dma_start(
                            out=where[:, :], out_offset=bass.IndirectOffsetOnAxis(ap=lidx[:, 0, c:c + 1], axis=0),
                            in_=lidx[:, 1, c:c + 1], in_offset=None,
                            bounds_check=NPAD - 1, oob_is_err=False).then_inc(l_scattered, 16)

                    def tiles(i, gathers_next):
                        for u in range(STREAMS):
                            rstd(ve_ready[u], 2 * i + 1, ve_[u], rs_[u], rs_ready[u])
                        locate(i, 0)
                        keep(0, i, 0)
                        locate(i, 1)
                        keep(1, i, 0)
                        rstd(ve_e, i + 1, eve, ers, rs_e)
                        locate(i, 2)
                        keep(0, i, 1)
                        locate(i, 3)
                        if gathers_next:
                            gather(i + 1, (0, 1))
                        keep(1, i, 1)
                        if gathers_next:
                            gather(i + 1, (4, 5))
                        keep(0, i, 2)
                        if gathers_next:
                            gather(i + 1, (2, 3))
                        keep(1, i, 2)
                        if gathers_next:
                            gather(i + 1, (6, 7))
                        for u in range(STREAMS):
                            rstd(ve_ready[u], 2 * i + 2, ve_[u], rs_[u], rs_ready[u])

                    gather(0, range(2 * CH))
                    with pool.Fori(0, ET - 1) as i:
                        tiles(i, True)
                    tiles(ET - 1, False)
                    pool.wait_ge(l_scattered, 64 * ET)

                @block.scalar
                def _(act):
                    def gates(u, i, s):
                        k = 3 * i + s
                        act.wait_ge(r_full[u], k + 1)
                        act.wait_ge(t1_ready[u], k)
                        nc.scalar.activation(r_[u][:, :], gate_bank[u][0][:, :], ACT.Sigmoid, bias=b_r).then_inc(r_ready[u], 1)
                        act.wait_ge(z_full[u], k + 1)
                        act.wait_ge(m_ready[u], k)
                        act.wait_ge(zh_ready[u], k)
                        nc.scalar.activation(z_[u][:, :], gate_bank[u][1][:, :], ACT.Sigmoid, bias=b_z).then_inc(z_ready[u], 1)
                        act.wait_ge(t1_ready[u], k + 1)
                        nc.scalar.activation(n_[u][:, :], t1_[u][:, :], ACT.Tanh, bias=b("ih_n")).then_inc(n_ready[u], 1)

                    def h_rows(u, i, s):
                        act.wait_ge(hr_stored[u], 32 * i + 16 * s)
                        act.wait_ge(misc_full[u], use(u, f"h{s + 1}", i) + 1)
                        nc.scalar.activation(hr_[u][:, :, :].rearrange("p c f -> p (c f)"), misc[u][:, :],
                                             ACT.Copy).then_inc(hr_ready[u], 1)

                    with act.Fori(0, ET) as i:
                        for u in range(STREAMS):
                            act.wait_ge(misc_full[u], use(u, "xT", i) + 1)
                            nc.scalar.activation(xT[u][:, :], misc[u][:, :], ACT.Copy).then_inc(xT_ready[u], 1)
                        act.wait_ge(misc_full[0], use(0, "dfT", i) + 1)
                        act.wait_ge(ef_ready, i)
                        nc.scalar.activation(dfT[:, :], misc[0][:, :], ACT.Copy).then_inc(dfT_ready, 1)
                        act.wait_ge(misc_full[1], use(1, "xdT", i) + 1)
                        nc.scalar.activation(xdT[:, :], misc[1][:, :], ACT.Copy).then_inc(xdT_ready, 1)
                        for u in range(STREAMS):
                            act.wait_ge(misc_full[u], use(u, "mlp", i) + 1)
                            act.wait_ge(y_ready[u], i)
                            nc.scalar.activation(relu_[u][:, :, :].rearrange("p c f -> p (c f)"), misc[u][:, :],
                                                 ACT.Relu).then_inc(relu_ready[u], 1)
                        act.wait_ge(misc_full[0], use(0, "pre", i) + 1)
                        nc.scalar.activation(erelu[:, :], misc[0][:, :], ACT.Relu, bias=b("edge")).then_inc(pre_ready, 1)
                        for u in range(STREAMS):
                            act.wait_ge(misc_full[u], use(u, "x1T", i) + 1)
                            act.wait_ge(fin_full[u], i)
                            nc.scalar.activation(x1T[u][:, :], misc[u][:, :], ACT.Copy).then_inc(x1T_ready[u], 1)
                        for u in range(STREAMS):
                            gates(u, i, 0)
                        act.wait_ge(misc_full[1], use(1, "emlp", i) + 1)
                        act.wait_ge(ey_ready, i)
                        nc.scalar.activation(emlp[:, :, :].rearrange("p c f -> p (c f)"), misc[1][:, :],
                                             ACT.Relu).then_inc(emlp_ready, 1)
                        h_rows(0, i, 0)
                        gates(0, i, 1)
                        h_rows(1, i, 0)
                        gates(1, i, 1)
                        act.wait_ge(misc_full[1], use(1, "ex1T", i) + 1)
                        act.wait_ge(ex1_stored, 32 * i)
                        nc.scalar.activation(ex1T[:, :], misc[1][:, :], ACT.Copy).then_inc(ex1T_ready, 1)
                        h_rows(0, i, 1)
                        gates(0, i, 2)
                        h_rows(1, i, 1)
                        gates(1, i, 2)
                        for u in range(STREAMS):
                            act.wait_ge(fin_full[u], i + 1)
                            act.wait_ge(fin_ready[u], i)
                            nc.scalar.activation(gate_[u][:, :, :].rearrange("p c f -> p (c f)"), gate_bank[u][0][:, :],
                                                 ACT.Sigmoid).then_inc(gate_ready[u], 1)

                @block.vector
                def _(v):
                    def norm(y_t, st, mv, ve, rs, o, seq, k, ve_done, rs_done, ready, free):
                        for c in range(CH):
                            ins = nc.vector.bn_stats(st[:, c, :], y_t[:, c, :])
                        ins.then_inc(seq, 1)
                        v.wait_ge(seq, 2 * k + 1)
                        v.sem_inc(v_passed, 1)
                        for c in range(CH):
                            ins = nc.vector.bn_aggr(mv[:, c, :], st[:, c, :])
                        ins.then_inc(seq, 1)
                        v.wait_ge(seq, 2 * k + 2)
                        nc.vector.tensor_scalar(ve[:, :], mv[:, :, 1], LN_EPS, None, ALU.add).then_inc(ve_done, 1)
                        for s_, v_ in free:
                            v.wait_ge(s_, v_)
                        v.wait_ge(rs_done, k + 1)
                        for c in range(CH):
                            ins = nc.vector.tensor_scalar(o[:, c, :], y_t[:, c, :], mv[:, c, 0:1], rs[:, c:c + 1],
                                                          ALU.subtract, ALU.mult)
                        ins.then_inc(ready, 1)

                    def step(u, i, s):
                        k = 3 * i + s
                        v.wait_ge(hn_full[u], k + 1)
                        v.wait_ge(r_ready[u], k + 1)
                        v.wait_ge(n_ready[u], k)
                        nc.vector.scalar_tensor_tensor(t1_[u][:, :], gate_bank[u][2][:, :], b("hh_n"), r_[u][:, :],
                                                       ALU.add, ALU.mult).then_inc(t1_ready[u], 1)
                        v.wait_ge(n_ready[u], k + 1)
                        v.wait_ge(z_ready[u], k + 1)
                        nc.vector.scalar_tensor_tensor(m_[u][:, :], z_[u][:, :], 1.0, n_[u][:, :],
                                                       ALU.subtract, ALU.mult).then_inc(m_ready[u], 1)
                        v.wait_ge(m_ready[u], k + 1)
                        v.wait_ge(zh_ready[u], k + 1)
                        if s == 0:
                            v.wait_ge(fin_full[u], i)
                        nc.vector.tensor_tensor(h_[u][:, :], zh_[u][:, :], m_[u][:, :], ALU.subtract).then_inc(h_ready[u], 1)

                    nc.vector.memset(carry[:, :], 0.0).then_inc(carry_ready, 1)
                    with v.Fori(0, ET) as i:
                        v.wait_ge(e_gathered, 128 * i + 128)
                        nc.vector.tensor_tensor(df[:, :, :], xd[:, :, :], xs[:, :, :], ALU.subtract).then_inc(df_ready, 1)
                        for u in range(STREAMS):
                            v.wait_ge(relu_ready[u], i + 1)
                            nc.vector.scalar_tensor_tensor(y[u][:, :, :], xr[u][:, :, :], 2.0, relu_[u][:, :, :],
                                                           ALU.mult, ALU.add).then_inc(y_ready[u], 1)
                            v.wait_ge(y_ready[u], i + 1)
                            norm(y[u], st_[u], mv_[u], ve_[u], rs_[u], x1r[u], st_ready[u], 2 * i, ve_ready[u],
                                 rs_ready[u], x1_ready[u], [(x1_stored[u], 16 * i)])
                        v.wait_ge(pre_ready, i + 1)
                        nc.vector.tensor_tensor(ef[:, :], erelu[:, :], dfT[:, :], ALU.add).then_inc(ef_ready, 1)
                        v.wait_ge(ef_ready, i + 1)
                        v.wait_ge(carry_ready, i + 1)
                        v.wait_ge(e_aux, 32 * i + 32)
                        v.wait_ge(emlp_ready, i)
                        nc.vector.tensor_tensor_scan(emax[:, :], restart[:, :], ef[:, :], carry[:, :],
                                                     ALU.add, ALU.max).then_inc(emax_ready, 1)
                        v.wait_ge(emax_ready, i + 1)
                        nc.vector.tensor_copy(carry[:, :], emax[:, TILE - 1:TILE]).then_inc(carry_ready, 1)
                        for u in range(STREAMS):
                            step(u, i, 0)
                        v.wait_ge(emlp_ready, i + 1)
                        nc.vector.scalar_tensor_tensor(ey[:, :, :], xd[:, :, :], 2.0, emlp[:, :, :],
                                                       ALU.mult, ALU.add).then_inc(ey_ready, 1)
                        v.wait_ge(ey_ready, i + 1)
                        norm(ey, est, emv, eve, ers, ex1r, e_stat, i, ve_e, rs_e, ex1_ready, [(ex1_stored, 32 * i)])
                        for s in range(1, STEPS):
                            for u in range(STREAMS):
                                step(u, i, s)
                        for u in range(STREAMS):
                            v.wait_ge(gate_ready[u], i + 1)
                            nc.vector.tensor_tensor(fin_[u][:, :, :].rearrange("p c f -> p (c f)"),
                                                    gate_bank[u][1][:, :],
                                                    gate_[u][:, :, :].rearrange("p c f -> p (c f)"),
                                                    ALU.mult).then_inc(fin_ready[u], 1)
                            v.wait_ge(fin_ready[u], i + 1)
                            nc.vector.tensor_tensor(yo_[u][:, :, :], fin_[u][:, :, :], x1r[u][:, :, :],
                                                    ALU.add).then_inc(yo_ready[u], 1)
                            v.wait_ge(yo_ready[u], i + 1)
                            norm(yo_[u], st_[u], mv_[u], ve_[u], rs_[u], or_[u], st_ready[u], 2 * i + 1, ve_ready[u],
                                 rs_ready[u], out_ready[u], [(out_stored[u], 16 * i)])

                @block.tensor
                def _(pe):
                    def gates(u, i, s):
                        k = 3 * i + s
                        h = x1T[u] if s == 0 else h_[u]
                        if s == 0:
                            pe.wait_ge(x1T_ready[u], i + 1)
                            pe.wait_ge(gate_ready[u], i)
                            pe.wait_ge(fin_ready[u], i)
                        else:
                            pe.wait_ge(h_ready[u], k)
                        bank = gate_bank[u]
                        product(bank[0][:, :], "hh_r", h[:, :], True, True).then_inc(r_full[u], 1)
                        product(bank[2][:, :], "hh_n", h[:, :], True, True).then_inc(hn_full[u], 1)
                        product(bank[1][:, :], "hh_z", h[:, :], True, True).then_inc(z_full[u], 1)

                    def h_rows(u, i, s):
                        if s == 0:
                            pe.wait_ge((x1T_ready[0], emlp_ready)[u], i + 1)
                        elif u == 0:
                            pe.wait_ge(hr_ready[0], 2 * i + 1)
                        else:
                            pe.wait_ge(ex1T_ready, i + 1)
                        pe.wait_ge(h_ready[u], 3 * i + s + 1)
                        flip(misc[u], chunks(h_[u][:, :])).then_inc(misc_full[u], 1)

                    with pe.Fori(0, ET) as i:
                        for u in range(STREAMS):
                            pe.wait_ge(x_loaded[u], 16 * i + 16)
                            pe.wait_ge(hr_ready[u], 2 * i)
                            flip(misc[u], xr[u]).then_inc(misc_full[u], 1)
                        pe.wait_ge(df_ready, i + 1)
                        pe.wait_ge(xT_ready[0], i + 1)
                        flip(misc[0], df).then_inc(misc_full[0], 1)
                        pe.wait_ge(e_gathered, 128 * i + 128)
                        pe.wait_ge(xT_ready[1], i + 1)
                        flip(misc[1], xd).then_inc(misc_full[1], 1)
                        for u in range(STREAMS):
                            pe.wait_ge(xT_ready[u], i + 1)
                            pe.wait_ge((dfT_ready, xdT_ready)[u], i + 1)
                            row_product(misc[u], [(xT[u], "mlp_x")], "mlp").then_inc(misc_full[u], 1)
                        pe.wait_ge(dfT_ready, i + 1)
                        pe.wait_ge(e_aux, 32 * i + 32)
                        pe.wait_ge(relu_ready[0], i + 1)
                        product(misc[0][:, :], "edge_x", dfT[:, :], True, False)
                        product(misc[0][:, :], "edge_f", efT[:, :], False, True, rows=F_E).then_inc(misc_full[0], 1)
                        for u in range(STREAMS):
                            pe.wait_ge(x1_ready[u], i + 1)
                            pe.wait_ge((pre_ready, relu_ready[1])[u], i + 1)
                            flip(misc[u], x1r[u]).then_inc(misc_full[u], 1)
                        for u in range(STREAMS):
                            gates(u, i, 0)
                        pe.wait_ge(xdT_ready, i + 1)
                        pe.wait_ge(emax_ready, i + 1)
                        pe.wait_ge(x1T_ready[1], i + 1)
                        row_product(misc[1], [(xdT, "mlp_x"), (emax, "mlp_m")], "mlp").then_inc(misc_full[1], 1)
                        h_rows(0, i, 0)
                        gates(0, i, 1)
                        h_rows(1, i, 0)
                        gates(1, i, 1)
                        pe.wait_ge(ex1_ready, i + 1)
                        pe.wait_ge(hr_ready[1], 2 * i + 1)
                        flip(misc[1], ex1r).then_inc(misc_full[1], 1)
                        h_rows(0, i, 1)
                        gates(0, i, 2)
                        h_rows(1, i, 1)
                        gates(1, i, 2)
                        for u in range(STREAMS):
                            pe.wait_ge(h_ready[u], 3 * i + STEPS)
                            row_product(gate_bank[u][0], [(h_[u], "i_h"), (x1T[u], "i_x")], "i")
                            row_product(gate_bank[u][1], [(h_[u], "j")], "j").then_inc(fin_full[u], 1)

        with ExitStack() as own:
            def sbo(name, shape, dt=F32):
                return own.enter_context(nc.sbuf_tensor(name, shape, dt))

            def two(name, shape, dt=F32):
                return [sbo(f"{name}{k}", shape, dt) for k in range(2)]

            rows = [P, CH, P]
            cols = [P, TILE]
            idx, at, seg = two("idx", [P, CH], I32), two("at", [P, CH], I32), two("seg", [P, CH], I32)
            g, h, hn_, same, mask = (two(n, s_, d) for n, s_, d in (
                ("g", rows, F32), ("h", cols, F32), ("hn_", cols, F32), ("same", cols, BF16), ("mask", [P, KT - 1, TILE], U8)))
            x1r, x1T = two("fx1r", rows), two("fx1T", cols)
            g_hi, g_lo, a_hi, a_lo, h_hi, h_lo = (sbo(n, cols, F32R) for n in ("g_hi", "g_lo", "a_hi", "a_lo", "h_hi", "h_lo"))
            msg, a, r_, z_, n_, t1_, t2_, zh_, m_ = (sbo(n, cols) for n in (
                "msg", "a", "er_", "ez_", "en_", "et1_", "et2_", "ezh_", "em_"))
            acarry = sbo("acarry", [P, 1])
            hrow, gate_, fin_, yo_, or_ = (sbo(n, rows) for n in ("hrow", "fgate", "ffin", "fyo", "for_"))
            st_, mv_, ve_, rs_ = sbo("fst", [P, CH, 6]), sbo("fmv", [P, CH, 2]), sbo("fve", [P, CH]), sbo("frs", [P, CH])
            gT_bank, t_bank, row_bank = banks[0], [banks[1], banks[2]], banks[3]
            r_bank, z_bank, hn_bank, in_bank = banks[4:8]

            (idx_loaded, at_gathered, at_stored, gathered, aux_loaded, h_loaded, h_stored, x1_loaded, seg_loaded,
             f_scattered) = (sems(f"a_{n}") for n in (
                 "idx_loaded at_gathered at_stored gathered aux_loaded h_loaded h_stored x1_loaded seg_loaded "
                 "f_scattered").split())
            (gT_full, g_hi_ready, g_lo_ready, t_full, msg_ready, a_ready, a_hi_ready, a_lo_ready, acarry_ready,
             h_hi_ready, h_lo_ready, r_full, hn_full, in_full, z_full, r_ready, z_ready, n_ready,
             t1_ready, t2_ready, zh_ready, m_ready, hn_ready, row_full, hrow_ready) = (sem(f"a_{n}") for n in (
                 "gT_full g_hi_ready g_lo_ready t_full msg_ready a_ready a_hi_ready a_lo_ready acarry_ready "
                 "h_hi_ready h_lo_ready r_full hn_full in_full z_full r_ready z_ready n_ready "
                 "t1_ready t2_ready zh_ready m_ready hn_ready row_full hrow_ready").split())
            (gate_full, j_full, gate_ready, fin_ready, yo_ready, f_stat, ve_ready, rs_ready, f_ready) = (
                sem(f"f_{n}") for n in "gate_full j_full gate_ready fin_ready yo_ready f_stat ve_ready rs_ready f_ready".split())

            OF_PARITY = [(ET + 1) // 2, ET // 2]
            flat = "p c f -> p (c f)"

            def tile_of(t, i):
                return t[bass.ds(i, 1), :, :].rearrange("t p c -> (t p) c")

            class Tile:
                def __init__(self, pair, odd):
                    self.n, self.half, self.par = pair * 2 + odd, pair + odd // 2, odd % 2
                    self.pair, self.odd = pair, odd

                def __add__(self, k):
                    return Tile(self.pair, self.odd + k)

                def of_parity(self, s):
                    return self.half + s * OF_PARITY[self.par]

            def exists(i):
                return not isinstance(i.n, int) or i.n < ET

            def pipeline(eng, ahead, body):
                ahead(Tile(0, 0))
                body(Tile(0, 0), None, True)
                body(Tile(0, 1), Tile(0, 0), True)
                with eng.Fori(1, ET // 2 - 1) as q:
                    for odd in range(2):
                        body(Tile(q, odd), Tile(q, odd - 1), True)
                for odd in range(2):
                    body(Tile(ET // 2 - 1, odd), Tile(ET // 2 - 1, odd - 1), True)
                body(Tile(ET // 2, 0), Tile(ET // 2, -1), False)
                body(None, Tile(ET // 2, 0), False)

            for s in range(STEPS):
                n = s * ET
                final = s == STEPS - 1
                with nc.Block() as block:
                    @block.sync
                    def _(sp):
                        def load_a(i):
                            u = i.par
                            if s == 0:
                                freed(sp, at_gathered[u], 64 * i.half)
                                sp.sem_inc(sp_passed, 1)
                                sp.dma_start(idx[u][:, :], tile_of(src_t, i.n)).then_inc(idx_loaded[u], 16)
                            else:
                                freed(sp, gathered[u], 64 * i.of_parity(s))
                                sp.dma_start(at[u][:, :], tile_of(src_rows, i.n)).then_inc(idx_loaded[u], 16)

                        def load_aux(i):
                            u = i.par
                            freed(sp, a_ready, n + i.n - 1)
                            sp.dma_start(mask[u][:, :, :], mask_d[:, bass.ds(i.n * TILE, TILE)].unsqueeze(0)
                                         .to_broadcast([P, KT - 1, TILE])).then_inc(aux_loaded[u], 16)
                            sp.dma_start(same[u][:, :], same_d[:, bass.ds(i.n * TILE, TILE)]
                                         .to_broadcast([P, TILE])).then_inc(aux_loaded[u], 16)

                        def load_b(j):
                            u = j.par
                            freed(sp, hn_ready, n + j.n - 1)
                            sp.dma_start(h[u][:, :], tile_of(states[s], j.n)).then_inc(h_loaded[u], 16)
                            if final:
                                freed(sp, yo_ready, j.n - 1)
                                sp.dma_start(x1r[u][:, :, :], edge_rows(tables[0], j.n)).then_inc(x1_loaded[u], 16)
                                sp.dma_start(x1T[u][:, :], tile_of(states[0], j.n)).then_inc(x1_loaded[u], 16)
                                freed(sp, f_scattered[u], 64 * j.half)
                                sp.sem_inc(sp_passed, 1)
                                sp.dma_start(seg[u][:, :], tile_of(last_t, j.n)).then_inc(seg_loaded[u], 16)

                        def ahead(i):
                            load_a(i)
                            if s == 0:
                                load_a(i + 1)
                            load_aux(i)
                            load_b(i)

                        def body(i, j, more):
                            if i is not None and s == 0:
                                sp.wait_ge(at_gathered[i.par], 64 * (i.half + 1))
                                sp.sem_inc(sp_passed, 1)
                                sp.dma_start(tile_of(src_rows, i.n), at[i.par][:, :]).then_inc(at_stored[i.par], 16)
                                if exists(i + 2):
                                    load_a(i + 2)
                            elif more:
                                load_a(i + 1)
                            if more:
                                load_aux(i + 1)
                                load_b(i + 1)
                            if j is not None and not final:
                                u = j.par
                                sp.wait_ge(hrow_ready, n + j.n + 1)
                                sp.dma_start(edge_rows(tables[s + 1], j.n), hrow[:, :, :]).then_inc(h_stored[u], 16)
                                sp.dma_start(tile_of(states[s + 1], j.n), hn_[u][:, :]).then_inc(h_stored[u], 16)

                        pipeline(sp, ahead, body)
                        for u in range(2):
                            if not final:
                                sp.wait_ge(h_stored[u], 32 * (s + 1) * OF_PARITY[u])
                            if s == 0:
                                sp.wait_ge(at_stored[u], 16 * OF_PARITY[u])

                    @block.gpsimd
                    def _(pool):
                        def find(i):
                            u = i.par
                            freed(pool, at_stored[u], 16 * i.half)
                            freed(pool, gathered[u], 64 * i.half)
                            pool.wait_ge(idx_loaded[u], 16 * (i.half + 1))
                            pool.sem_inc(passed, 1)
                            for c in range(CH):
                                nc.gpsimd.indirect_dma_start(
                                    out=at[u][:, c:c + 1], out_offset=None, in_=where[:, :],
                                    in_offset=bass.IndirectOffsetOnAxis(ap=idx[u][:, c:c + 1], axis=0),
                                    bounds_check=NPAD - 1, oob_is_err=False).then_inc(at_gathered[u], 16)

                        def gather(i):
                            u, k = i.par, i.of_parity(s)
                            if s == 0:
                                pool.wait_ge(at_gathered[u], 64 * (i.half + 1))
                            else:
                                pool.wait_ge(idx_loaded[u], 16 * (k + 1))
                            freed(pool, gT_full, n + i.n - 1)
                            pool.sem_inc(passed, 1)
                            for c in range(CH):
                                nc.gpsimd.indirect_dma_start(
                                    out=g[u][:, c, :], out_offset=None, in_=tables[s][:, :],
                                    in_offset=bass.IndirectOffsetOnAxis(ap=at[u][:, c:c + 1], axis=0),
                                    bounds_check=NPAD + EPAD - 1, oob_is_err=False).then_inc(gathered[u], 16)

                        def ahead(i):
                            if s == 0:
                                find(i)
                                find(i + 1)
                            gather(i)

                        def body(i, j, more):
                            if more:
                                gather(i + 1)
                            if j is not None:
                                u = j.par
                                pool.wait_ge(h_loaded[u], 16 * (j.of_parity(s) + 1))
                                pool.wait_ge(z_ready, n + j.n + 1)
                                freed(pool, hn_ready, n + j.n)
                                nc.gpsimd.tensor_tensor(zh_[:, :], z_[:, :], h[u][:, :], ALU.mult).then_inc(zh_ready, 1)
                            if s == 0 and i is not None and exists(i + 2):
                                find(i + 2)
                            if final and j is not None:
                                pool.wait_ge(ve_ready, j.n + 1)
                                nc.gpsimd.tensor_tensor(rs_[:, :], ve_[:, :], half[:, :], ALU.pow).then_inc(rs_ready, 1)
                                pool.wait_ge(f_ready, j.n + 1)
                                pool.wait_ge(seg_loaded[u], 16 * (j.half + 1))
                                pool.sem_inc(passed, 1)
                                for c in range(CH):
                                    nc.gpsimd.indirect_dma_start(
                                        out=out[:, :], out_offset=bass.IndirectOffsetOnAxis(ap=seg[u][:, c:c + 1], axis=0),
                                        in_=or_[:, c, :], in_offset=None,
                                        bounds_check=NPAD - 1, oob_is_err=False).then_inc(f_scattered[u], 16)

                        pipeline(pool, ahead, body)
                        if final:
                            for u in range(2):
                                pool.wait_ge(f_scattered[u], 64 * OF_PARITY[u])

                    @block.scalar
                    def _(act):
                        def ahead(i):
                            pass

                        def split_h(j):
                            act.wait_ge(h_loaded[j.par], 16 * (j.of_parity(s) + 1))
                            freed(act, z_full, n + j.n)
                            freed(act, h_lo_ready, n + j.n)
                            nc.scalar.activation(h_hi[:, :], h[j.par][:, :], ACT.Copy).then_inc(h_hi_ready, 1)

                        def body(i, j, more):
                            if i is not None:
                                act.wait_ge(gT_full, n + i.n + 1)
                                freed(act, t_full, KT * (n + i.n))
                                nc.scalar.activation(g_hi[:, :], gT_bank[:, :], ACT.Copy).then_inc(g_hi_ready, 1)
                            if j is not None:
                                act.wait_ge(r_full, n + j.n + 1)
                                freed(act, t1_ready, n + j.n)
                                nc.scalar.activation(r_[:, :], r_bank[:, :], ACT.Sigmoid, bias=b_r).then_inc(r_ready, 1)
                                act.wait_ge(z_full, n + j.n + 1)
                                freed(act, m_ready, n + j.n)
                                freed(act, zh_ready, n + j.n)
                                nc.scalar.activation(z_[:, :], z_bank[:, :], ACT.Sigmoid, bias=b_z).then_inc(z_ready, 1)
                                act.wait_ge(t2_ready, n + j.n + 1)
                                nc.scalar.activation(n_[:, :], t2_[:, :], ACT.Tanh, bias=b("ih_n")).then_inc(n_ready, 1)
                            if i is not None:
                                act.wait_ge(t_full, KT * (n + i.n) + 1)
                                freed(act, a_ready, n + i.n)
                                nc.scalar.activation(msg[:, :], t_bank[0][:, :], ACT.Identity, bias=b("et0")).then_inc(msg_ready, 1)
                                split_h(i)
                            if j is not None:
                                if final:
                                    act.wait_ge(gate_full, j.n + 1)
                                    freed(act, fin_ready, j.n)
                                    nc.scalar.activation(gate_[:, :, :].rearrange(flat), row_bank[:, :],
                                                         ACT.Sigmoid).then_inc(gate_ready, 1)
                                else:
                                    act.wait_ge(row_full, n + j.n + 1)
                                    last = j + (-1)
                                    freed(act, h_stored[last.par], 32 * (last.of_parity(s) + 1))
                                    nc.scalar.activation(hrow[:, :, :].rearrange(flat), row_bank[:, :],
                                                         ACT.Copy).then_inc(hrow_ready, 1)
                            if i is not None:
                                act.wait_ge(a_ready, n + i.n + 1)
                                freed(act, z_full, n + i.n)
                                freed(act, a_lo_ready, n + i.n)
                                nc.scalar.activation(a_hi[:, :], a[:, :], ACT.Copy).then_inc(a_hi_ready, 1)

                        pipeline(act, ahead, body)

                    @block.vector
                    def _(v):
                        def ahead(i):
                            nc.vector.memset(acarry[:, :], 0.0).then_inc(acarry_ready, 1)

                        def body(i, j, more):
                            if i is not None:
                                v.wait_ge(g_hi_ready, n + i.n + 1)
                                freed(v, t_full, KT * (n + i.n))
                                nc.vector.tensor_tensor(g_lo[:, :], gT_bank[:, :], g_hi[:, :].bitcast(F32),
                                                        ALU.subtract).then_inc(g_lo_ready, 1)
                            if j is not None:
                                u = j.par
                                v.wait_ge(hn_full, n + j.n + 1)
                                v.wait_ge(r_ready, n + j.n + 1)
                                nc.vector.scalar_tensor_tensor(t1_[:, :], hn_bank[:, :], b("hh_n"), r_[:, :],
                                                               ALU.add, ALU.mult).then_inc(t1_ready, 1)
                                v.wait_ge(in_full, n + j.n + 1)
                                v.wait_ge(t1_ready, n + j.n + 1)
                                freed(v, n_ready, n + j.n)
                                nc.vector.tensor_tensor(t2_[:, :], in_bank[:, :], t1_[:, :], ALU.add).then_inc(t2_ready, 1)
                                v.wait_ge(n_ready, n + j.n + 1)
                                v.wait_ge(z_ready, n + j.n + 1)
                                nc.vector.scalar_tensor_tensor(m_[:, :], z_[:, :], 1.0, n_[:, :],
                                                               ALU.subtract, ALU.mult).then_inc(m_ready, 1)
                                v.wait_ge(m_ready, n + j.n + 1)
                                v.wait_ge(zh_ready, n + j.n + 1)
                                if final:
                                    freed(v, j_full, j.n)
                                else:
                                    freed(v, h_stored[u], 32 * j.of_parity(s))
                                nc.vector.tensor_tensor(hn_[u][:, :], zh_[:, :], m_[:, :], ALU.subtract).then_inc(hn_ready, 1)
                            if i is not None:
                                u = i.par
                                v.wait_ge(h_hi_ready, n + i.n + 1)
                                freed(v, z_full, n + i.n)
                                nc.vector.tensor_tensor(h_lo[:, :], h[u][:, :], h_hi[:, :].bitcast(F32),
                                                        ALU.subtract).then_inc(h_lo_ready, 1)
                                v.wait_ge(aux_loaded[u], 32 * (i.of_parity(s) + 1))
                                for k in range(1, KT):
                                    v.wait_ge(msg_ready, KT * (n + i.n) + k)
                                    v.wait_ge(t_full, KT * (n + i.n) + k + 1)
                                    v.sem_inc(v_passed, 1)
                                    nc.vector.copy_predicated(msg[:, :], mask[u][:, k - 1, :], t_bank[k % 2][:, :]).then_inc(msg_ready, 1)
                                v.wait_ge(msg_ready, KT * (n + i.n) + KT)
                                v.wait_ge(acarry_ready, n + s + i.n + 1)
                                freed(v, a_hi_ready, n + i.n)
                                nc.vector.tensor_tensor_scan(a[:, :], same[u][:, :], msg[:, :], acarry[:, :],
                                                             ALU.mult, ALU.add).then_inc(a_ready, 1)
                                v.wait_ge(a_ready, n + i.n + 1)
                                nc.vector.tensor_copy(acarry[:, :], a[:, TILE - 1:TILE]).then_inc(acarry_ready, 1)
                                v.wait_ge(a_hi_ready, n + i.n + 1)
                                nc.vector.tensor_tensor(a_lo[:, :], a[:, :], a_hi[:, :].bitcast(F32),
                                                        ALU.subtract).then_inc(a_lo_ready, 1)
                            if j is not None and final:
                                u = j.par
                                v.wait_ge(gate_ready, j.n + 1)
                                v.wait_ge(j_full, j.n + 1)
                                nc.vector.tensor_tensor(fin_[:, :, :].rearrange(flat), r_bank[:, :],
                                                        gate_[:, :, :].rearrange(flat), ALU.mult).then_inc(fin_ready, 1)
                                v.wait_ge(fin_ready, j.n + 1)
                                v.wait_ge(x1_loaded[u], 32 * (j.half + 1))
                                nc.vector.tensor_tensor(yo_[:, :, :], fin_[:, :, :], x1r[u][:, :, :], ALU.add).then_inc(yo_ready, 1)
                                v.wait_ge(yo_ready, j.n + 1)
                                for c in range(CH):
                                    ins = nc.vector.bn_stats(st_[:, c, :], yo_[:, c, :])
                                ins.then_inc(f_stat, 1)
                                v.wait_ge(f_stat, 2 * j.n + 1)
                                v.sem_inc(v_passed, 1)
                                for c in range(CH):
                                    ins = nc.vector.bn_aggr(mv_[:, c, :], st_[:, c, :])
                                ins.then_inc(f_stat, 1)
                                v.wait_ge(f_stat, 2 * j.n + 2)
                                nc.vector.tensor_scalar(ve_[:, :], mv_[:, :, 1], LN_EPS, None, ALU.add).then_inc(ve_ready, 1)
                                last = j + (-1)
                                freed(v, f_scattered[last.par], 64 * (last.half + 1))
                                v.wait_ge(rs_ready, j.n + 1)
                                for c in range(CH):
                                    ins = nc.vector.tensor_scalar(or_[:, c, :], yo_[:, c, :], mv_[:, c, 0:1], rs_[:, c:c + 1],
                                                                  ALU.subtract, ALU.mult)
                                ins.then_inc(f_ready, 1)

                        pipeline(v, ahead, body)

                    @block.tensor
                    def _(pe):
                        def ahead(i):
                            pass

                        def body(i, j, more):
                            if i is not None:
                                pe.wait_ge(gathered[i.par], 64 * (i.of_parity(s) + 1))
                                freed(pe, g_lo_ready, n + i.n)
                                flip(gT_bank, g[i.par]).then_inc(gT_full, 1)
                            if j is not None:
                                pe.wait_ge(h_lo_ready, n + j.n + 1)
                                if final:
                                    freed(pe, fin_ready, j.n)
                                product3(hn_bank, "hh_n", h_hi, h_lo, True, True).then_inc(hn_full, 1)
                                product3(r_bank, "hh_r", h_hi, h_lo, True, False)
                                product3(z_bank, "hh_z", h_hi, h_lo, True, False)
                                pe.wait_ge(a_lo_ready, n + j.n + 1)
                                product3(r_bank, "ih_r", a_hi, a_lo, False, True).then_inc(r_full, 1)
                                freed(pe, t2_ready, n + j.n)
                                product3(in_bank, "ih_n", a_hi, a_lo, True, True).then_inc(in_full, 1)
                                product3(z_bank, "ih_z", a_hi, a_lo, False, True).then_inc(z_full, 1)
                            if i is not None:
                                pe.wait_ge(g_lo_ready, n + i.n + 1)
                                freed(pe, a_ready, n + i.n)
                                for k in range(KT):
                                    if k >= 2:
                                        pe.wait_ge(msg_ready, KT * (n + i.n) + k - 1)
                                    mm = product3(t_bank[k % 2], f"et{k}", g_hi, g_lo, True, k == 0)
                                    if k:
                                        mm = bias_cols(t_bank[k % 2][:, :], f"et{k}")
                                    mm.then_inc(t_full, 1)
                            if j is not None:
                                pe.wait_ge(hn_ready, n + j.n + 1)
                                if final:
                                    pe.wait_ge(x1_loaded[j.par], 32 * (j.half + 1))
                                    freed(pe, gate_ready, j.n)
                                    row_product(row_bank, [(hn_[j.par], "i_h"), (x1T[j.par], "i_x")], "i").then_inc(gate_full, 1)
                                    row_product(r_bank, [(hn_[j.par], "j")], "j").then_inc(j_full, 1)
                                else:
                                    freed(pe, hrow_ready, n + j.n)
                                    flip(row_bank, chunks(hn_[j.par][:, :])).then_inc(row_full, 1)

                        pipeline(pe, ahead, body)


def kernel(**inputs):
    import numpy as np
    import concourse.bacc as bacc
    from concourse.bass_utils import run_bass_kernel_spmd

    q = {k: np.asarray(v) for k, v in inputs.items()}
    x = np.zeros((NPAD, P), np.float32)
    x[:N] = q["x"]
    dst = np.full(EPAD + 2, N, np.int32)
    dst[0] = -1
    dst[1:E + 1] = q["dst"]
    src = np.full(EPAD, N, np.int32)
    src[:E] = q["src"]
    kind = np.zeros(EPAD, np.int32)
    kind[:E] = q["edge_type_4"]
    ef = np.zeros((EPAD, F_E), np.float32)
    ef[:E] = q["edge_attr_64"]

    def by_chunk(a):
        return np.ascontiguousarray(a.reshape(ET, CH, P).transpose(0, 2, 1))

    def linear(a):
        return np.ascontiguousarray(a.reshape(P, ECOL))

    we = np.zeros((2 * P, P), np.float32)
    we[:P + F_E] = q["L0_gnn_W_edge"]
    wm, iw = q["L0_gnn_W_mlp"], q["L1_gnn_i_w"].T
    parts = [we[:P], we[P:], wm[:P], wm[P:]] + [q["L1_gnn_W_et"][k].T for k in range(KT)]
    parts += [q["L1_gnn_W_ih"][k * P:(k + 1) * P].T for k in range(3)]
    parts += [q["L1_gnn_W_hh"][k * P:(k + 1) * P].T for k in range(3)]
    parts += [iw[:P], iw[P:], q["L1_gnn_j_w"].T]
    cols = [q["L0_gnn_b_edge"]] + [q["L1_gnn_b_et"][k] for k in range(KT)]
    cols += [q["L1_gnn_b_ih"][k * P:(k + 1) * P] for k in range(3)]
    cols += [q["L1_gnn_b_hh"][k * P:(k + 1) * P] for k in range(3)]
    brows = [q["L0_gnn_b_mlp"], q["L1_gnn_i_b"], q["L1_gnn_j_b"]] + [q["L1_gnn_b_et"][k] for k in range(KT)]
    arrays = {
        "x_rows": x,
        "dst_lin": linear(dst[1:-1]), "prev_lin": linear(dst[:-2]), "type_lin": linear(kind),
        "dst_t": by_chunk(dst[1:-1]), "next_t": by_chunk(dst[2:]), "src_t": by_chunk(src),
        "ef_t": np.ascontiguousarray(ef.T),
        "weights": np.ascontiguousarray(np.concatenate(parts, axis=1)),
        "biases": np.ascontiguousarray(np.stack(cols, axis=1)),
        "bias_rows": np.ascontiguousarray(np.concatenate(brows).reshape(1, -1)),
    }
    nc = bacc.Bacc("TRN2", target_bir_lowering=False, num_devices=1)
    args = [nc.dram_tensor(k, a.shape, mybir.dt.from_np(a.dtype), kind="ExternalInput").ap() for k, a in arrays.items()]
    out = nc.dram_tensor("out_rows", (NPAD, P), F32, kind="ExternalOutput").ap()
    build(nc, *args, out)
    r = run_bass_kernel_spmd(nc, [arrays], core_ids=[0])
    return r.results[0]["out_rows"][:N]
```

```python
from contextlib import ExitStack

import concourse.bass as bass
from concourse import mybir

P = 128
N = 50000
E = 25000
CH = 4
TILE = P * CH
ET = -(-E // TILE)
EPAD = ET * TILE
NT = -(-N // TILE)
NPAD = NT * TILE
ECOL = EPAD // P
KT = 4
F_E = 64
STEPS = 3
STREAMS = 2
NOWHERE = 1 << 20
LN_EPS = 1e-5
RESTART = -3.0e38
assert NT == STREAMS * ET and ET % 2 == 1

ALU = mybir.AluOpType
ACT = mybir.ActivationFunctionType
F32 = mybir.dt.float32
BF16 = mybir.dt.bfloat16
F32R = mybir.dt.float32r
I32 = mybir.dt.int32
U8 = mybir.dt.uint8

W_NAMES = (["edge_x", "edge_f", "mlp_x", "mlp_m"] + [f"et{k}" for k in range(KT)]
           + ["ih_r", "ih_z", "ih_n", "hh_r", "hh_z", "hh_n", "i_h", "i_x", "j"])
W3_NAMES = [f"et{k}" for k in range(KT)] + ["ih_r", "ih_z", "ih_n", "hh_r", "hh_z", "hh_n"]
W3_FROM = W_NAMES.index(W3_NAMES[0])
assert W_NAMES[W3_FROM:W3_FROM + len(W3_NAMES)] == W3_NAMES
PARTS = 3
B_NAMES = ["edge"] + [f"et{k}" for k in range(KT)] + ["ih_r", "ih_z", "ih_n", "hh_r", "hh_z", "hh_n"]
ROW_BIASES = ["mlp", "i", "j"]
R_NAMES = ROW_BIASES + [f"et{k}" for k in range(KT)]


def freed(eng, semaphore, value):
    if not (isinstance(value, int) and value <= 0):
        eng.wait_ge(semaphore, value)


def build(nc, x, dst_lin, prev_lin, type_lin, dst_cols, next_cols, src_cols, ef_t, weights, biases, bias_rows, out):
    with ExitStack() as ctx:
        def sb(name, shape, dt=F32):
            return ctx.enter_context(nc.sbuf_tensor(name, shape, dt))

        def sem(name):
            return ctx.enter_context(nc.semaphore(name))

        def sems(name, n=STREAMS):
            return [sem(f"{name}{k}") for k in range(n)]

        def dram(name, shape, dt=F32):
            return nc.dram_tensor(name, shape, dt, kind="Internal").ap()

        tables = [dram(f"table{s}", (NPAD + EPAD, P)) for s in range(STEPS)]
        states = [dram(f"state{s}", (ET, P, TILE)) for s in range(STEPS)]
        where = dram("where", (NPAD, 1), I32)
        same_d = dram("same_d", (1, EPAD), BF16)
        restart_d = dram("restart_d", (1, EPAD), BF16)
        mask_d = dram("mask_d", (KT - 1, EPAD), U8)

        wt = sb("wt", [P, len(W_NAMES) * P])
        bs = sb("bs", [P, len(B_NAMES)])
        brz = sb("brz", [P, 2])
        bpart = sb("bpart", [PARTS, len(R_NAMES) * P], BF16)
        brows = sb("brows", [PARTS, len(ROW_BIASES) * TILE], BF16)
        ones = sb("ones", [PARTS, TILE], BF16)
        w_hi, w_lo = (sb(n, [P, len(W3_NAMES) * P], F32R) for n in ("w_hi", "w_lo"))
        ident = sb("ident", [P, P])
        minus_half = sb("minus_half", [P, CH])
        dst_all, src_all, last_all, rows_all = (sb(n, [P, ECOL], I32) for n in ("dst_all", "src_all", "last_all", "rows_all"))

        def w(name, rows=P):
            k = W_NAMES.index(name)
            return wt[0:rows, k * P:(k + 1) * P]

        def b(name):
            k = B_NAMES.index(name)
            return bs[:, k:k + 1]

        b_r, b_z = brz[:, 0:1], brz[:, 1:2]

        passed, v_passed, sp_passed = sem("passed"), sem("v_passed"), sem("sp_passed")

        banks = [ctx.enter_context(nc.psum_tensor(f"bank{k}", [P, TILE], F32)) for k in range(8)]

        def product(o, name, operand, first, last, rows=P):
            return nc.tensor.matmul(o, w(name, rows), operand, start=first, stop=last)

        def product3(bank, name, hi, lo, first, last):
            k = W3_NAMES.index(name) * P
            nc.tensor.matmul(bank[:, :], w_hi[:, k:k + P], hi[:, :], start=first, stop=False)
            nc.tensor.matmul(bank[:, :], w_hi[:, k:k + P], lo[:, :], start=False, stop=False)
            return nc.tensor.matmul(bank[:, :], w_lo[:, k:k + P], hi[:, :], start=False, stop=last)

        def bias_rows_into(bank, name):
            k = R_NAMES.index(name)
            nc.tensor.matmul(bank[:, :], ones[:, 0:P], brows[:, k * TILE:(k + 1) * TILE], start=True, stop=False)

        def bias_cols(o, name):
            k = R_NAMES.index(name) * P
            return nc.tensor.matmul(o, bpart[:, k:k + P], ones[:, :], start=False, stop=True)

        def flip(o, rows):
            for c in range(CH):
                mm = nc.tensor.transpose(o[:, c * P:(c + 1) * P], rows[:, c, :], ident[:, :])
            return mm

        def chunks(t):
            return t.rearrange("p (c f) -> p c f", c=CH)

        def row_product(bank, terms, bias):
            bias_rows_into(bank, bias)
            for c in range(CH):
                for n, (operand, name) in enumerate(terms):
                    mm = nc.tensor.matmul(bank[:, c * P:(c + 1) * P], operand[:, c * P:(c + 1) * P], w(name),
                                          start=False, stop=(c, n) == (CH - 1, len(terms) - 1))
            return mm

        def node_rows(table, t):
            return table[bass.ds(t * TILE, TILE), :].rearrange("(p c) f -> p c f", c=CH)

        def edge_rows(table, t):
            return table[bass.ds(t * TILE + NPAD, TILE), :].rearrange("(c p) f -> p c f", p=P)

        def tile_of(t, i):
            return t[bass.ds(i, 1), :, :].rearrange("t p c -> (t p) c")

        with ExitStack() as own:
            def sbo(name, shape, dt=I32):
                return own.enter_context(nc.sbuf_tensor(name, shape, dt))

            dl, pl, tl = sbo("dl", [P, ECOL]), sbo("pl", [P, ECOL]), sbo("tl", [P, ECOL])
            next_all = sbo("next_all", [P, ECOL])
            same_s, restart_s = sbo("same_s", [P, ECOL], BF16), sbo("restart_s", [P, ECOL], BF16)
            mask_s = sbo("mask_s", [P, KT - 1, ECOL], U8)
            more = sbo("more", [P, ECOL])
            where_s = sbo("where_s", [P, NPAD // P])
            brow, bres, bsum = (sbo(n, [PARTS, len(R_NAMES) * P], F32) for n in ("brow", "bres", "bsum"))
            bcut = sbo("bcut", [PARTS, len(R_NAMES) * P], BF16)
            indices_loaded, loaded, pool_ready = sem("indices_loaded"), sem("loaded"), sem("pool_ready")
            part, flags_ready = sem("part"), sem("flags_ready")
            setup_stored = sem("setup_stored")

            with nc.Block() as block:
                @block.sync
                def _(sp):
                    for t, d in ((dl, dst_lin), (pl, prev_lin), (tl, type_lin),
                                 (dst_all, dst_cols), (next_all, next_cols), (src_all, src_cols)):
                        sp.dma_start(t[:, :], d).then_inc(indices_loaded, 16)
                    sp.dma_start(brow[:, :], bias_rows.to_broadcast([PARTS, len(R_NAMES) * P])).then_inc(loaded, 16)
                    sp.dma_start(bs[:, :], biases).then_inc(loaded, 16)
                    sp.dma_start(wt[:, :], weights).then_inc(loaded, 16)
                    sp.wait_ge(pool_ready, 5)
                    sp.dma_start(where.rearrange("(p c) o -> p (c o)", p=P), where_s[:, :]).then_inc(setup_stored, 16)
                    sp.wait_ge(flags_ready, 1)
                    sp.dma_start(same_d.rearrange("o (p c) -> (o p) c", p=P), same_s[:, :]).then_inc(setup_stored, 16)
                    sp.dma_start(restart_d.rearrange("o (p c) -> (o p) c", p=P), restart_s[:, :]).then_inc(setup_stored, 16)
                    sp.dma_start(mask_d.rearrange("k (p c) -> p k c", p=P), mask_s[:, :, :]).then_inc(setup_stored, 16)
                    sp.wait_ge(setup_stored, 64)

                @block.gpsimd
                def _(pool):
                    nc.gpsimd.memset(ident[:, :], 0.0).then_inc(pool_ready, 1)
                    pool.wait_ge(pool_ready, 1)
                    nc.gpsimd.affine_select(out=ident[:, :], in_=ident[:, :], compare_op=ALU.not_equal, fill=1.0,
                                            base=0, pattern=[[-1, P]], channel_multiplier=1).then_inc(pool_ready, 1)
                    nc.gpsimd.memset(minus_half[:, :], -0.5).then_inc(pool_ready, 1)
                    nc.gpsimd.iota(where_s[:, :], pattern=[[1, NPAD // P]], base=0,
                                   channel_multiplier=NPAD // P).then_inc(pool_ready, 1)
                    nc.gpsimd.iota(rows_all[:, :], pattern=[[P, ECOL]], base=NPAD,
                                   channel_multiplier=1).then_inc(pool_ready, 1)

                @block.vector
                def _(v):
                    made = [0]

                    def made_by(ins):
                        made[0] += 1
                        ins.then_inc(part, 1)

                    v.wait_ge(indices_loaded, 96)
                    made_by(nc.vector.tensor_tensor(same_s[:, :], dl[:, :], pl[:, :], ALU.is_equal))
                    v.wait_ge(part, made[0])
                    made_by(nc.vector.tensor_scalar(restart_s[:, :], same_s[:, :], -1.0, -RESTART, ALU.add, ALU.mult))
                    for k in range(1, KT):
                        made_by(nc.vector.tensor_scalar(mask_s[:, k - 1, :], tl[:, :], float(k), None, ALU.is_equal))
                    made_by(nc.vector.tensor_tensor(more[:, :], dst_all[:, :], next_all[:, :], ALU.is_equal))
                    v.wait_ge(part, made[0])
                    nc.vector.scalar_tensor_tensor(last_all[:, :], more[:, :], float(NOWHERE), dst_all[:, :],
                                                   ALU.mult, ALU.add).then_inc(flags_ready, 1)
                    nc.vector.memset(ones[:, :], 1.0)
                    v.wait_ge(loaded, 48)
                    made_by(nc.vector.tensor_tensor(brz[:, 0:1], b("ih_r"), b("hh_r"), ALU.add))
                    made_by(nc.vector.tensor_tensor(brz[:, 1:2], b("ih_z"), b("hh_z"), ALU.add))
                    v.wait_ge(pool_ready, 5)
                    for n in range(PARTS):
                        from_ = brow if n == 0 else bres
                        v.wait_ge(part, made[0])
                        made_by(nc.vector.tensor_copy(bcut[:, :], from_[:, :]))
                        v.wait_ge(part, made[0])
                        if n == 0:
                            made_by(nc.vector.tensor_scalar(bsum[:, :], bcut[:, :], ident[0:PARTS, n:n + 1], None, ALU.mult))
                        else:
                            made_by(nc.vector.scalar_tensor_tensor(bsum[:, :], bcut[:, :], ident[0:PARTS, n:n + 1], bsum[:, :],
                                                                   ALU.mult, ALU.add))
                        made_by(nc.vector.tensor_tensor(bres[:, :], from_[:, :], bcut[:, :], ALU.subtract))
                    v.wait_ge(part, made[0])
                    made_by(nc.vector.tensor_copy(bpart[:, :], bsum[:, :]))
                    v.wait_ge(part, made[0])
                    for k in range(len(ROW_BIASES)):
                        for c in range(CH):
                            made_by(nc.vector.tensor_copy(brows[:, k * TILE + c * P:k * TILE + (c + 1) * P],
                                                          bpart[:, k * P:(k + 1) * P]))
                    split = wt[:, W3_FROM * P:(W3_FROM + len(W3_NAMES)) * P]
                    made_by(nc.vector.tensor_copy(w_hi[:, :], split))
                    v.wait_ge(part, made[0])
                    made_by(nc.vector.tensor_tensor(w_lo[:, :], split, w_hi[:, :].bitcast(F32), ALU.subtract))

        with ExitStack() as own:
            def sbo(name, shape, dt=F32):
                return own.enter_context(nc.sbuf_tensor(name, shape, dt))

            def two(name, shape, dt=F32):
                return [sbo(f"{name}{u}", shape, dt) for u in range(2)]

            rows = [P, CH, P]
            cols = [P, TILE]
            flat = "p c f -> p (c f)"
            xr, xT, relu_, y = (two(n, s) for n, s in (("xr", rows), ("xT", cols), ("relu_", rows), ("y", rows)))
            r_, z_, n_, t1_, zh_, m_, h_ = (two(n, cols) for n in ("r_", "z_", "n_", "t1_", "zh_", "m_", "h_"))
            hr_, gate_, fin_, yo_, or_ = (two(n, rows) for n in ("hr_", "gate_", "fin_", "yo_", "or_"))
            x1r, x1T = [two(f"x1r{k}", rows) for k in range(2)], [two(f"x1T{k}", cols) for k in range(2)]
            xd, xs = two("xd", rows), two("xs", rows)
            eidx = two("eidx", [P, 2, CH], I32)
            lidx = sbo("lidx", [P, 2, CH], I32)
            df = sbo("df", rows)
            dfT, xdT, erelu, ef, emax = (sbo(n, cols) for n in ("dfT", "xdT", "erelu", "ef", "emax"))
            efT, restart = sbo("efT", [F_E, TILE]), sbo("restart", cols, BF16)
            carry = sbo("carry", [P, 1])
            emlp, ey, ex1r, ex1T = sbo("emlp", rows), sbo("ey", rows), sbo("ex1r", rows), sbo("ex1T", cols)

            gate_bank = [banks[0:3], banks[3:6]]
            misc = banks[6:8]

            x_loaded, xT_full, xT_ready, mlp_full, relu_ready, y_ready = (sems(n) for n in (
                "x_loaded", "xT_full", "xT_ready", "mlp_full", "relu_ready", "y_ready"))
            x1_ready, x1T_full, x1T_ready, x1_stored = (sems(n) for n in ("x1_ready", "x1T_full", "x1T_ready", "x1_stored"))
            r_full, hn_full, z_full = sems("r_full"), sems("hn_full"), sems("z_full")
            r_ready, z_ready, n_ready = sems("r_ready"), sems("z_ready"), sems("n_ready")
            t1_ready, zh_ready, m_ready, h_ready = sems("t1_ready"), sems("zh_ready"), sems("m_ready"), sems("h_ready")
            hr_full, hr_ready, hr_stored = sems("hr_full"), sems("hr_ready"), sems("hr_stored")
            fin_full, gate_ready, fin_ready, yo_ready = sems("fin_full"), sems("gate_ready"), sems("fin_ready"), sems("yo_ready")
            out_ready, out_stored, e_gathered = sems("out_ready"), sems("out_stored"), sems("e_gathered")
            (l_scattered, e_picked, l_picked, df_ready, eT_full, eT_ready, ef_loaded,
             restart_loaded, pre_full, pre_ready, ef_ready, emax_ready, carry_ready, emlp_full, emlp_ready, ey_ready,
             ex1_ready, ex1T_full, ex1T_ready, ex1_stored) = (sem(n) for n in (
                 "l_scattered e_picked l_picked df_ready eT_full eT_ready ef_loaded "
                 "restart_loaded pre_full pre_ready ef_ready emax_ready carry_ready emlp_full emlp_ready ey_ready "
                 "ex1_ready ex1T_full ex1T_ready ex1_stored").split())


            def h_bank(s, u):
                return misc[1] if (s, u) == (0, 0) else misc[0]

            class Norm:
                def __init__(self, name):
                    self.st, self.mv = sbo(f"st_{name}", [P, CH, 6]), sbo(f"mv_{name}", [P, CH, 2])
                    self.ve, self.rs = sbo(f"ve_{name}", [P, CH]), sbo(f"rs_{name}", [P, CH])
                    self.nm, self.shift = sbo(f"nm_{name}", [P, CH]), sbo(f"shift_{name}", [P, CH])
                    self.counted, self.rs_ready = sem(f"counted_{name}"), sem(f"rs_ready_{name}")

            x1_norm, out_norm, e_norm = [Norm(f"x{u}") for u in range(2)], [Norm(f"o{u}") for u in range(2)], Norm("e")

            class Round:
                def __init__(self, pair, odd):
                    self.n, self.par, self.half = pair * 2 + odd, odd % 2, pair + odd // 2

                def node_tile(self, u):
                    return self.n * STREAMS + u

            def rounds(eng, front, body):
                front(Round(0, 0))
                body(Round(0, 0), Round(0, 1), None)
                body(Round(0, 1), Round(0, 2), Round(0, 0))
                with eng.Fori(1, ET // 2 - 1) as q:
                    body(Round(q, 0), Round(q, 1), Round(q, -1))
                    body(Round(q, 1), Round(q, 2), Round(q, 0))
                body(Round(ET // 2, -2), Round(ET // 2, -1), Round(ET // 2, -3))
                body(Round(ET // 2, -1), Round(ET // 2, 0), Round(ET // 2, -2))
                body(Round(ET // 2, 0), None, Round(ET // 2, -1))
                body(None, None, Round(ET // 2, 0))

            with nc.Block() as block:
                @block.sync
                def _(sp):
                    def load_x(t, u):
                        freed(sp, y_ready[u], t.n)
                        sp.dma_start(xr[u][:, :, :], node_rows(x, t.node_tile(u))).then_inc(x_loaded[u], 16)

                    def load_edge_features(t):
                        freed(sp, pre_full, t.n)
                        sp.dma_start(efT[:, :], ef_t[:, bass.ds(t.n * TILE, TILE)]).then_inc(ef_loaded, 16)

                    def load_restart(t):
                        freed(sp, emax_ready, t.n)
                        sp.sem_inc(sp_passed, 1)
                        sp.dma_start(restart[:, :], restart_d[:, bass.ds(t.n * TILE, TILE)].to_broadcast([P, TILE])).then_inc(restart_loaded, 16)

                    def store_x1(t, u):
                        sp.wait_ge(x1_ready[u], t.n + 1)
                        sp.dma_start(node_rows(tables[0], t.node_tile(u)), x1r[t.par][u][:, :, :]).then_inc(x1_stored[u], 16)

                    def store_h(t, s, u):
                        sp.wait_ge(hr_ready[u], 2 * t.n + s + 1)
                        sp.dma_start(node_rows(tables[s + 1], t.node_tile(u)), hr_[u][:, :, :]).then_inc(hr_stored[u], 16)

                    def store_out(t, u):
                        sp.wait_ge(out_ready[u], t.n + 1)
                        sp.dma_start(node_rows(out, t.node_tile(u)), or_[u][:, :, :]).then_inc(out_stored[u], 16)

                    def front(t):
                        load_x(t, 0)
                        load_x(t, 1)
                        load_edge_features(t)
                        load_restart(t)
                        for u in range(STREAMS):
                            load_x(Round(0, 1), u)
                            store_x1(t, u)

                    def body(i, n, p):
                        if p is not None:
                            store_out(p, 0)
                            store_out(p, 1)
                        if i is None:
                            return
                        two_on = n is not None and not (isinstance(n.n, int) and n.n + 1 >= ET)
                        after = two_on and Round(n.half, n.par + 1)
                        store_h(i, 0, 0)
                        if two_on:
                            load_x(after, 0)
                        if n is not None:
                            load_edge_features(n)
                        store_h(i, 0, 1)
                        if n is not None:
                            load_restart(n)
                        if two_on:
                            load_x(after, 1)
                        if n is not None:
                            store_x1(n, 0)
                            store_x1(n, 1)
                        store_h(i, 1, 0)
                        store_h(i, 1, 1)
                        sp.wait_ge(ex1_ready, i.n + 1)
                        sp.dma_start(edge_rows(tables[0], i.n), ex1r[:, :, :]).then_inc(ex1_stored, 16)
                        sp.wait_ge(ex1T_ready, i.n + 1)
                        sp.dma_start(tile_of(states[0], i.n), ex1T[:, :]).then_inc(ex1_stored, 16)

                    rounds(sp, front, body)
                    for u in range(STREAMS):
                        sp.wait_ge(x1_stored[u], 16 * ET)
                        sp.wait_ge(hr_stored[u], 32 * ET)
                        sp.wait_ge(out_stored[u], 16 * ET)
                    sp.wait_ge(ex1_stored, 32 * ET)

                @block.gpsimd
                def _(pool):
                    def rstd(norm, t, shift=True):
                        pool.wait_ge(norm.counted, 3 * t.n + 3)
                        nc.gpsimd.tensor_tensor(norm.rs[:, :], norm.ve[:, :], minus_half[:, :], ALU.pow).then_inc(norm.rs_ready, 1)
                        if shift:
                            pool.wait_ge(norm.rs_ready, 2 * t.n + 1)
                            nc.gpsimd.tensor_tensor(norm.shift[:, :], norm.nm[:, :], norm.rs[:, :], ALU.mult).then_inc(norm.rs_ready, 1)

                    def keep(i, s, u):
                        pool.wait_ge(z_ready[u], 3 * i.n + s + 1)
                        freed(pool, h_ready[u], 3 * i.n + s)
                        h = x1T[i.par][u] if s == 0 else h_[u]
                        nc.gpsimd.tensor_tensor(zh_[u][:, :], z_[u][:, :], h[:, :], ALU.mult).then_inc(zh_ready[u], 1)

                    def pick(t, arrays, n, picked):
                        for k, a in enumerate(arrays):
                            nc.gpsimd.tensor_copy(t[:, k, :], a[:, bass.ds(n * CH, CH)]).then_inc(picked, 1)
                        pool.wait_ge(picked, 2 * n + 2)

                    def gather(t, cs):
                        if 0 in cs:
                            freed(pool, e_gathered[t.par], 128 * t.half)
                            pick(eidx[t.par], (dst_all, src_all), t.n, e_picked)
                            freed(pool, ey_ready, t.n - 1)
                            pool.sem_inc(passed, 1)
                        for c in cs:
                            for k, to in enumerate((xd, xs)):
                                nc.gpsimd.indirect_dma_start(
                                    out=to[t.par][:, c, :], out_offset=None, in_=x[:, :],
                                    in_offset=bass.IndirectOffsetOnAxis(ap=eidx[t.par][:, k, c:c + 1], axis=0),
                                    bounds_check=NPAD - 1, oob_is_err=False).then_inc(e_gathered[t.par], 16)

                    def locate(t, cs):
                        if 0 in cs:
                            freed(pool, l_scattered, 64 * t.n)
                            pick(lidx, (last_all, rows_all), t.n, l_picked)
                            pool.sem_inc(passed, 1)
                        for c in cs:
                            nc.gpsimd.indirect_dma_start(
                                out=where[:, :], out_offset=bass.IndirectOffsetOnAxis(ap=lidx[:, 0, c:c + 1], axis=0),
                                in_=lidx[:, 1, c:c + 1], in_offset=None,
                                bounds_check=NPAD - 1, oob_is_err=False).then_inc(l_scattered, 16)

                    def front(t):
                        gather(t, range(CH))
                        rstd(x1_norm[0], t)
                        rstd(x1_norm[1], t)

                    def body(i, n, p):
                        if i is None:
                            rstd(out_norm[0], p)
                            rstd(out_norm[1], p)
                            return
                        if n is not None:
                            gather(n, (0,))
                        keep(i, 0, 0)
                        if p is not None:
                            rstd(out_norm[0], p)
                        locate(i, (0, 1))
                        keep(i, 0, 1)
                        if p is not None:
                            rstd(out_norm[1], p)
                        if n is not None:
                            gather(n, (1,))
                        keep(i, 1, 0)
                        if n is not None:
                            rstd(x1_norm[0], n)
                            gather(n, (2,))
                        keep(i, 1, 1)
                        if n is not None:
                            rstd(x1_norm[1], n)
                        keep(i, 2, 0)
                        if n is not None:
                            gather(n, (3,))
                        rstd(e_norm, i, shift=False)
                        keep(i, 2, 1)
                        locate(i, (2, 3))

                    rounds(pool, front, body)
                    pool.wait_ge(l_scattered, 64 * ET)

                @block.scalar
                def _(act):
                    def copy(o, bank, ready, func=ACT.Copy):
                        nc.scalar.activation(o, bank[:, :], func).then_inc(ready, 1)

                    def gates(i, s, u):
                        k = 3 * i.n + s
                        act.wait_ge(r_full[u], k + 1)
                        freed(act, t1_ready[u], k)
                        nc.scalar.activation(r_[u][:, :], gate_bank[u][0][:, :], ACT.Sigmoid, bias=b_r).then_inc(r_ready[u], 1)
                        act.wait_ge(z_full[u], k + 1)
                        freed(act, m_ready[u], k)
                        freed(act, zh_ready[u], k)
                        nc.scalar.activation(z_[u][:, :], gate_bank[u][1][:, :], ACT.Sigmoid, bias=b_z).then_inc(z_ready[u], 1)
                        if (s, u) == (1, 0):
                            act.wait_ge(eT_full, 2 * i.n + 2)
                            freed(act, emlp_full, i.n)
                            copy(xdT[:, :], misc[0], eT_ready)
                        act.wait_ge(t1_ready[u], k + 1)
                        nc.scalar.activation(n_[u][:, :], t1_[u][:, :], ACT.Tanh, bias=b("ih_n")).then_inc(n_ready[u], 1)

                    def h_rows(i, s, u):
                        act.wait_ge(hr_full[u], 2 * i.n + s + 1)
                        freed(act, hr_stored[u], 32 * i.n + 16 * s)
                        copy(hr_[u][:, :, :].rearrange(flat), h_bank(s, u), hr_ready[u])

                    def apply(norm, t, values, o, ready):
                        act.wait_ge(norm.rs_ready, 2 * t.n + 2)
                        for c in range(CH):
                            ins = nc.scalar.activation(o[:, c, :], values[:, c, :], ACT.Identity,
                                                       bias=norm.shift[:, c:c + 1], scale=norm.rs[:, c:c + 1])
                        ins.then_inc(ready, 1)

                    def x1_rows(t, u):
                        freed(act, x1_stored[u], 16 * (t.n - 1))
                        freed(act, yo_ready[u], t.n - 1)
                        apply(x1_norm[u], t, y[u], x1r[t.par][u], x1_ready[u])

                    def out_rows(t, u):
                        freed(act, out_stored[u], 16 * t.n)
                        apply(out_norm[u], t, yo_[u], or_[u], out_ready[u])

                    def gate(t, u):
                        act.wait_ge(fin_full[u], t.n + 1)
                        freed(act, fin_ready[u], t.n)
                        copy(gate_[u][:, :, :].rearrange(flat), gate_bank[u][0], gate_ready[u], ACT.Sigmoid)

                    def transposed_x(t, u):
                        act.wait_ge(xT_full[u], t.n + 1)
                        freed(act, mlp_full[u], t.n)
                        copy(xT[u][:, :], misc[u], xT_ready[u])

                    def relu(t, u):
                        act.wait_ge(mlp_full[u], t.n + 1)
                        freed(act, y_ready[u], t.n)
                        copy(relu_[u][:, :, :].rearrange(flat), misc[0], relu_ready[u], ACT.Relu)

                    def transposed_x1(t, u):
                        act.wait_ge(x1T_full[u], t.n + 1)
                        freed(act, fin_full[u], t.n - 1)
                        copy(x1T[t.par][u][:, :], misc[1], x1T_ready[u])

                    def front(t):
                        transposed_x(t, 0)
                        transposed_x(t, 1)
                        relu(t, 0)
                        relu(t, 1)
                        x1_rows(t, 0)
                        x1_rows(t, 1)
                        transposed_x1(t, 0)
                        transposed_x1(t, 1)

                    def body(i, n, p):
                        if i is not None:
                            gates(i, 0, 0)
                        if p is not None:
                            gate(p, 1)
                        if i is None:
                            out_rows(p, 0)
                            out_rows(p, 1)
                            return
                        if n is not None:
                            transposed_x(n, 0)
                            transposed_x(n, 1)
                        gates(i, 0, 1)
                        if n is not None:
                            relu(n, 0)
                        act.wait_ge(eT_full, 2 * i.n + 1)
                        freed(act, ef_ready, i.n)
                        copy(dfT[:, :], misc[1], eT_ready)
                        if p is not None:
                            out_rows(p, 0)
                        gates(i, 1, 0)
                        act.wait_ge(pre_full, i.n + 1)
                        freed(act, ef_ready, i.n)
                        nc.scalar.activation(erelu[:, :], misc[1][:, :], ACT.Relu, bias=b("edge")).then_inc(pre_ready, 1)
                        if n is not None:
                            relu(n, 1)
                        h_rows(i, 0, 0)
                        if p is not None:
                            out_rows(p, 1)
                        gates(i, 1, 1)
                        h_rows(i, 0, 1)
                        if n is not None:
                            x1_rows(n, 0)
                        act.wait_ge(emlp_full, i.n + 1)
                        freed(act, ey_ready, i.n)
                        copy(emlp[:, :, :].rearrange(flat), misc[1], emlp_ready, ACT.Relu)
                        gates(i, 2, 0)
                        h_rows(i, 1, 0)
                        if n is not None:
                            x1_rows(n, 1)
                        if n is not None:
                            transposed_x1(n, 0)
                        gates(i, 2, 1)
                        h_rows(i, 1, 1)
                        gate(i, 0)
                        if n is not None:
                            transposed_x1(n, 1)
                        act.wait_ge(ex1T_full, i.n + 1)
                        freed(act, ex1_stored, 32 * i.n)
                        copy(ex1T[:, :], misc[0], ex1T_ready)

                    rounds(act, front, body)

                @block.vector
                def _(v):
                    def moments(norm, t, values):
                        for c in range(CH):
                            ins = nc.vector.bn_stats(norm.st[:, c, :], values[:, c, :])
                        ins.then_inc(norm.counted, 1)
                        v.wait_ge(norm.counted, 3 * t.n + 1)
                        v.sem_inc(v_passed, 1)
                        for c in range(CH):
                            ins = nc.vector.bn_aggr(norm.mv[:, c, :], norm.st[:, c, :])
                        ins.then_inc(norm.counted, 1)
                        v.wait_ge(norm.counted, 3 * t.n + 2)
                        nc.vector.tensor_scalar(norm.nm[:, :], norm.mv[:, :, 0], -1.0, None, ALU.mult)
                        nc.vector.tensor_scalar(norm.ve[:, :], norm.mv[:, :, 1], LN_EPS, None, ALU.add).then_inc(norm.counted, 1)

                    def t1(i, s, u):
                        k = 3 * i.n + s
                        v.wait_ge(hn_full[u], k + 1)
                        v.wait_ge(r_ready[u], k + 1)
                        freed(v, n_ready[u], k)
                        nc.vector.scalar_tensor_tensor(t1_[u][:, :], gate_bank[u][2][:, :], b("hh_n"), r_[u][:, :],
                                                       ALU.add, ALU.mult).then_inc(t1_ready[u], 1)

                    def m(i, s, u):
                        k = 3 * i.n + s
                        v.wait_ge(n_ready[u], k + 1)
                        v.wait_ge(z_ready[u], k + 1)
                        nc.vector.scalar_tensor_tensor(m_[u][:, :], z_[u][:, :], 1.0, n_[u][:, :],
                                                       ALU.subtract, ALU.mult).then_inc(m_ready[u], 1)

                    def h(i, s, u):
                        k = 3 * i.n + s
                        v.wait_ge(m_ready[u], k + 1)
                        v.wait_ge(zh_ready[u], k + 1)
                        if s == 0:
                            freed(v, fin_full[u], i.n)
                        else:
                            v.wait_ge(hr_full[u], 2 * i.n + s)
                        nc.vector.tensor_tensor(h_[u][:, :], zh_[u][:, :], m_[u][:, :], ALU.subtract).then_inc(h_ready[u], 1)

                    def residual(t, u):
                        v.wait_ge(x_loaded[u], 16 * (t.n + 1))
                        v.wait_ge(relu_ready[u], t.n + 1)
                        freed(v, x1_ready[u], t.n)
                        nc.vector.scalar_tensor_tensor(y[u][:, :, :], xr[u][:, :, :], 2.0, relu_[u][:, :, :],
                                                       ALU.mult, ALU.add).then_inc(y_ready[u], 1)

                    def x1_moments(t, u):
                        v.wait_ge(y_ready[u], t.n + 1)
                        moments(x1_norm[u], t, y[u])

                    def gated(t, u):
                        v.wait_ge(gate_ready[u], t.n + 1)
                        nc.vector.tensor_tensor(fin_[u][:, :, :].rearrange(flat), gate_bank[u][1][:, :],
                                                gate_[u][:, :, :].rearrange(flat), ALU.mult).then_inc(fin_ready[u], 1)

                    def out_moments(t, u):
                        v.wait_ge(fin_ready[u], t.n + 1)
                        freed(v, out_ready[u], t.n)
                        nc.vector.tensor_tensor(yo_[u][:, :, :], fin_[u][:, :, :], x1r[t.par][u][:, :, :],
                                                ALU.add).then_inc(yo_ready[u], 1)
                        v.wait_ge(yo_ready[u], t.n + 1)
                        moments(out_norm[u], t, yo_[u])

                    def front(t):
                        nc.vector.memset(carry[:, :], 0.0).then_inc(carry_ready, 1)
                        for u in range(STREAMS):
                            residual(t, u)
                            x1_moments(t, u)

                    def body(i, n, p):
                        if i is None:
                            gated(p, 1)
                            for u in range(STREAMS):
                                out_moments(p, u)
                            return
                        t1(i, 0, 0)
                        v.wait_ge(e_gathered[i.par], 128 * (i.half + 1))
                        nc.vector.tensor_tensor(df[:, :, :], xd[i.par][:, :, :], xs[i.par][:, :, :],
                                                ALU.subtract).then_inc(df_ready, 1)
                        m(i, 0, 0)
                        if p is not None:
                            out_moments(p, 0)
                        h(i, 0, 0)
                        if p is not None:
                            gated(p, 1)
                        t1(i, 0, 1)
                        if p is not None:
                            out_moments(p, 1)
                        m(i, 0, 1)
                        h(i, 0, 1)
                        t1(i, 1, 0)
                        if n is not None:
                            residual(n, 0)
                        m(i, 1, 0)
                        if n is not None:
                            x1_moments(n, 0)
                        h(i, 1, 0)
                        v.wait_ge(pre_ready, i.n + 1)
                        nc.vector.tensor_tensor(ef[:, :], erelu[:, :], dfT[:, :], ALU.add).then_inc(ef_ready, 1)
                        v.wait_ge(ef_ready, i.n + 1)
                        v.wait_ge(carry_ready, i.n + 1)
                        v.wait_ge(restart_loaded, 16 * (i.n + 1))
                        freed(v, emlp_full, i.n)
                        nc.vector.tensor_tensor_scan(emax[:, :], restart[:, :], ef[:, :], carry[:, :],
                                                     ALU.add, ALU.max).then_inc(emax_ready, 1)
                        v.wait_ge(emax_ready, i.n + 1)
                        nc.vector.tensor_copy(carry[:, :], emax[:, TILE - 1:TILE]).then_inc(carry_ready, 1)
                        t1(i, 1, 1)
                        m(i, 1, 1)
                        if n is not None:
                            residual(n, 1)
                        h(i, 1, 1)
                        if n is not None:
                            x1_moments(n, 1)
                        t1(i, 2, 0)
                        v.wait_ge(emlp_ready, i.n + 1)
                        nc.vector.scalar_tensor_tensor(ey[:, :, :], xd[i.par][:, :, :], 2.0, emlp[:, :, :],
                                                       ALU.mult, ALU.add).then_inc(ey_ready, 1)
                        m(i, 2, 0)
                        h(i, 2, 0)
                        v.wait_ge(ey_ready, i.n + 1)
                        moments(e_norm, i, ey)
                        t1(i, 2, 1)
                        freed(v, ex1_stored, 32 * i.n)
                        freed(v, ex1T_full, i.n)
                        v.wait_ge(e_norm.rs_ready, i.n + 1)
                        for c in range(CH):
                            ins = nc.vector.tensor_scalar(ex1r[:, c, :], ey[:, c, :], e_norm.mv[:, c, 0:1],
                                                          e_norm.rs[:, c:c + 1], ALU.subtract, ALU.mult)
                        ins.then_inc(ex1_ready, 1)
                        m(i, 2, 1)
                        h(i, 2, 1)
                        gated(i, 0)

                    rounds(v, front, body)

                @block.tensor
                def _(pe):
                    def gates(i, s, u):
                        k = 3 * i.n + s
                        h = x1T[i.par][u] if s == 0 else h_[u]
                        bank = gate_bank[u]
                        if s == 0:
                            pe.wait_ge(x1T_ready[u], i.n + 1)
                            freed(pe, gate_ready[u], i.n)
                        else:
                            pe.wait_ge(h_ready[u], k)
                        product(bank[0][:, :], "hh_r", h[:, :], True, True).then_inc(r_full[u], 1)
                        product(bank[2][:, :], "hh_n", h[:, :], True, True).then_inc(hn_full[u], 1)
                        if s == 0:
                            freed(pe, fin_ready[u], i.n)
                        product(bank[1][:, :], "hh_z", h[:, :], True, True).then_inc(z_full[u], 1)

                    def final(t, u):
                        pe.wait_ge(h_ready[u], 3 * t.n + STEPS)
                        row_product(gate_bank[u][0], [(h_[u], "i_h"), (x1T[t.par][u], "i_x")], "i")
                        row_product(gate_bank[u][1], [(h_[u], "j")], "j").then_inc(fin_full[u], 1)

                    def transpose_x(t, u):
                        pe.wait_ge(x_loaded[u], 16 * (t.n + 1))
                        flip(misc[u], xr[u]).then_inc(xT_full[u], 1)

                    def mlp(t, u):
                        pe.wait_ge(xT_ready[u], t.n + 1)
                        row_product(misc[0], [(xT[u], "mlp_x")], "mlp").then_inc(mlp_full[u], 1)

                    def transpose_x1(t, u):
                        pe.wait_ge(x1_ready[u], t.n + 1)
                        flip(misc[1], x1r[t.par][u]).then_inc(x1T_full[u], 1)

                    def transpose_h(s, u):
                        return flip(h_bank(s, u), chunks(h_[u][:, :])).then_inc(hr_full[u], 1)

                    def front(t):
                        transpose_x(t, 0)
                        transpose_x(t, 1)
                        mlp(t, 0)
                        pe.wait_ge(relu_ready[0], t.n + 1)
                        mlp(t, 1)
                        transpose_x1(t, 0)
                        pe.wait_ge(x1T_ready[0], t.n + 1)
                        transpose_x1(t, 1)

                    def body(i, n, p):
                        if i is not None:
                            gates(i, 0, 0)
                        if p is not None:
                            final(p, 1)
                        if i is None:
                            return
                        if n is not None:
                            if p is not None:
                                pe.wait_ge(ex1T_ready, i.n)
                            else:
                                pe.wait_ge(relu_ready[1], n.n)
                            transpose_x(n, 0)
                            pe.wait_ge(x1T_ready[1], n.n)
                            transpose_x(n, 1)
                        gates(i, 0, 1)
                        if n is not None:
                            mlp(n, 0)
                            pe.wait_ge(xT_ready[1], n.n + 1)
                        else:
                            pe.wait_ge(x1T_ready[1], i.n + 1)
                        pe.wait_ge(df_ready, i.n + 1)
                        flip(misc[1], df).then_inc(eT_full, 1)
                        gates(i, 1, 0)
                        pe.wait_ge(e_gathered[i.par], 128 * (i.half + 1))
                        if n is not None:
                            pe.wait_ge(relu_ready[0], n.n + 1)
                        else:
                            pe.wait_ge(ex1T_ready, i.n)
                        flip(misc[0], xd[i.par]).then_inc(eT_full, 1)
                        pe.wait_ge(eT_ready, 2 * i.n + 1)
                        pe.wait_ge(ef_loaded, 16 * (i.n + 1))
                        product(misc[1][:, :], "edge_x", dfT[:, :], True, False)
                        product(misc[1][:, :], "edge_f", efT[:, :], False, True, rows=F_E).then_inc(pre_full, 1)
                        pe.wait_ge(eT_ready, 2 * i.n + 2)
                        if n is not None:
                            mlp(n, 1)
                        pe.wait_ge(pre_ready, i.n + 1)
                        transpose_h(0, 0)
                        gates(i, 1, 1)
                        if n is not None:
                            pe.wait_ge(relu_ready[1], n.n + 1)
                        transpose_h(0, 1)
                        pe.wait_ge(hr_ready[0], 2 * i.n + 1)
                        pe.wait_ge(emax_ready, i.n + 1)
                        row_product(misc[1], [(xdT, "mlp_x"), (emax, "mlp_m")], "mlp").then_inc(emlp_full, 1)
                        gates(i, 2, 0)
                        pe.wait_ge(hr_ready[1], 2 * i.n + 1)
                        transpose_h(1, 0)
                        if n is not None:
                            pe.wait_ge(emlp_ready, i.n + 1)
                            transpose_x1(n, 0)
                        gates(i, 2, 1)
                        pe.wait_ge(hr_ready[0], 2 * i.n + 2)
                        transpose_h(1, 1)
                        final(i, 0)
                        if n is not None:
                            pe.wait_ge(x1T_ready[0], n.n + 1)
                            transpose_x1(n, 1)
                        pe.wait_ge(ex1_ready, i.n + 1)
                        pe.wait_ge(hr_ready[1], 2 * i.n + 2)
                        flip(misc[0], ex1r).then_inc(ex1T_full, 1)

                    rounds(pe, front, body)

        with ExitStack() as own:
            def sbo(name, shape, dt=F32):
                return own.enter_context(nc.sbuf_tensor(name, shape, dt))

            def two(name, shape, dt=F32):
                return [sbo(f"{name}{k}", shape, dt) for k in range(2)]

            rows = [P, CH, P]
            cols = [P, TILE]
            g, h, hn_, same, mask = (two(n, s_, d) for n, s_, d in (
                ("g", rows, F32), ("h", cols, F32), ("hn_", cols, F32), ("same", cols, BF16), ("mask", [P, KT - 1, TILE], U8)))
            x1r, x1T, or_ = two("fx1r", rows), two("fx1T", cols), two("for_", rows)
            h_hi, h_lo = two("h_hi", cols, F32R), two("h_lo", cols, F32R)
            g_hi, g_lo, a_hi, a_lo = (sbo(n, cols, F32R) for n in ("g_hi", "g_lo", "a_hi", "a_lo"))
            msg, a, r_, z_, n_, t1_, t2_, zh_, m_ = (sbo(n, cols) for n in (
                "msg", "a", "er_", "ez_", "en_", "et1_", "et2_", "ezh_", "em_"))
            acarry = sbo("acarry", [P, 1])
            hrow, gate_, fin_ = (sbo(n, rows) for n in ("hrow", "fgate", "ffin"))
            st_, mv_ = sbo("fst", [P, CH, 6]), sbo("fmv", [P, CH, 2])
            ve_, nm_ = sbo("fve", [P, CH]), sbo("fnm", [P, CH])
            yo_, rs_, shift_ = two("fyo", rows), two("frs", [P, CH]), two("fshift", [P, CH])
            idx, at, last = (two(n, [P, CH], I32) for n in ("idx", "at", "last"))
            at_all = sbo("at_all", [P, ECOL], I32)
            gT_bank, t_bank, row_bank = banks[0], [banks[1], banks[2]], banks[3]
            r_bank, z_bank, hn_bank, in_bank = banks[4:8]

            idx_picked, at_picked, at_kept, last_picked = (sem(n) for n in ("idx_picked", "at_picked", "at_kept", "last_picked"))
            (at_found, gathered, aux_loaded, h_loaded, h_stored, x1_loaded, f_scattered) = (sems(f"a_{n}") for n in (
                "at_found gathered aux_loaded h_loaded h_stored x1_loaded f_scattered").split())
            (gT_full, g_hi_ready, g_lo_ready, t_full, msg_ready, a_ready, a_hi_ready, a_lo_ready, acarry_ready,
             h_hi_ready, h_lo_ready, r_full, hn_full, in_full, z_full, r_ready, z_ready, n_ready,
             t1_ready, t2_ready, zh_ready, m_ready, hn_ready, row_full, hrow_ready) = (sem(f"a_{n}") for n in (
                 "gT_full g_hi_ready g_lo_ready t_full msg_ready a_ready a_hi_ready a_lo_ready acarry_ready "
                 "h_hi_ready h_lo_ready r_full hn_full in_full z_full r_ready z_ready n_ready "
                 "t1_ready t2_ready zh_ready m_ready hn_ready row_full hrow_ready").split())
            (gate_full, j_full, gate_ready, fin_ready, yo_ready, f_stat, ve_ready, rs_ready, f_ready) = (
                sem(f"f_{n}") for n in "gate_full j_full gate_ready fin_ready yo_ready f_stat ve_ready rs_ready f_ready".split())

            OF_PARITY = [(ET + 1) // 2, ET // 2]
            flat = "p c f -> p (c f)"

            class Tile:
                def __init__(self, pair, odd):
                    self.n, self.half, self.par = pair * 2 + odd, pair + odd // 2, odd % 2
                    self.pair, self.odd = pair, odd

                def __add__(self, k):
                    return Tile(self.pair, self.odd + k)

                def of_parity(self, s):
                    return self.half + s * OF_PARITY[self.par]

                def exists(self):
                    return not isinstance(self.n, int) or self.n < ET

            def pipeline(eng, ahead, body):
                ahead()

                def tile_round(pair, odd):
                    i = Tile(pair, odd)
                    is_int = isinstance(pair, int)
                    stages = [i + (-d) for d in range(3)]
                    body(*[t if not is_int or 0 <= t.n < ET else None for t in stages])

                for k in range(6):
                    tile_round(0, k)
                with eng.Fori(3, ET // 2 - 1) as q:
                    tile_round(q, 0)
                    tile_round(q, 1)
                for k in range(-2, 3):
                    tile_round(ET // 2, k)

            for s in range(STEPS):
                n = s * ET
                final = s == STEPS - 1
                keep_on_pool = s > 0

                def keep(eng, ops, j):
                    eng.wait_ge(h_loaded[j.par], 16 * (j.of_parity(s) + 1))
                    eng.wait_ge(z_ready, n + j.n + 1)
                    freed(eng, hn_ready, n + j.n)
                    ops.tensor_tensor(zh_[:, :], z_[:, :], h[j.par][:, :], ALU.mult).then_inc(zh_ready, 1)

                with nc.Block() as block:
                    @block.sync
                    def _(sp):
                        def load_aux(i):
                            u = i.par
                            freed(sp, a_ready, n + i.n - 1)
                            sp.dma_start(mask[u][:, :, :], mask_d[:, bass.ds(i.n * TILE, TILE)].unsqueeze(0)
                                         .to_broadcast([P, KT - 1, TILE])).then_inc(aux_loaded[u], 16)
                            sp.dma_start(same[u][:, :], same_d[:, bass.ds(i.n * TILE, TILE)]
                                         .to_broadcast([P, TILE])).then_inc(aux_loaded[u], 16)

                        def load_h(i):
                            freed(sp, hn_ready, n + i.n - 1)
                            sp.dma_start(h[i.par][:, :], tile_of(states[s], i.n)).then_inc(h_loaded[i.par], 16)

                        def load_x1(i):
                            u = i.par
                            freed(sp, yo_ready, i.n - 1)
                            sp.dma_start(x1r[u][:, :, :], edge_rows(tables[0], i.n)).then_inc(x1_loaded[u], 16)
                            sp.dma_start(x1T[u][:, :], tile_of(states[0], i.n)).then_inc(x1_loaded[u], 16)

                        def ahead():
                            load_aux(Tile(0, 0))
                            load_h(Tile(0, 0))

                        def body(i, j, k):
                            if i is not None and (i + 1).exists():
                                load_aux(i + 1)
                                load_h(i + 1)
                            if i is not None and final:
                                load_x1(i)
                            if j is not None and not final:
                                sp.wait_ge(hn_ready, n + j.n + 1)
                                sp.dma_start(tile_of(states[s + 1], j.n), hn_[j.par][:, :]).then_inc(h_stored[j.par], 16)
                                sp.wait_ge(hrow_ready, n + j.n + 1)
                                sp.dma_start(edge_rows(tables[s + 1], j.n), hrow[:, :, :]).then_inc(h_stored[j.par], 16)

                        pipeline(sp, ahead, body)
                        if not final:
                            for u in range(2):
                                sp.wait_ge(h_stored[u], 32 * (s + 1) * OF_PARITY[u])

                    @block.gpsimd
                    def _(pool):
                        def columns(i):
                            return bass.ds(i.n * CH, CH)

                        def find(i):
                            u = i.par
                            freed(pool, at_found[u], 64 * i.half)
                            nc.gpsimd.tensor_copy(idx[u][:, :], src_all[:, columns(i)]).then_inc(idx_picked, 1)
                            pool.wait_ge(idx_picked, i.n + 1)
                            freed(pool, at_kept, i.n - 1)
                            freed(pool, gathered[u], 64 * i.half)
                            pool.sem_inc(passed, 1)
                            for c in range(CH):
                                nc.gpsimd.indirect_dma_start(
                                    out=at[u][:, c:c + 1], out_offset=None, in_=where[:, :],
                                    in_offset=bass.IndirectOffsetOnAxis(ap=idx[u][:, c:c + 1], axis=0),
                                    bounds_check=NPAD - 1, oob_is_err=False).then_inc(at_found[i.par], 16)

                        def gather(i, cs):
                            u = i.par
                            if 0 in cs:
                                if s == 0:
                                    pool.wait_ge(at_found[u], 64 * (i.half + 1))
                                    nc.gpsimd.tensor_copy(at_all[:, columns(i)], at[u][:, :]).then_inc(at_kept, 1)
                                else:
                                    freed(pool, gathered[u], 64 * i.of_parity(s))
                                    nc.gpsimd.tensor_copy(at[u][:, :], at_all[:, columns(i)]).then_inc(at_picked, 1)
                                    pool.wait_ge(at_picked, n - ET + i.n + 1)
                                freed(pool, gT_full, n + i.n - 1)
                                pool.sem_inc(passed, 1)
                            for c in cs:
                                nc.gpsimd.indirect_dma_start(
                                    out=g[u][:, c, :], out_offset=None, in_=tables[s][:, :],
                                    in_offset=bass.IndirectOffsetOnAxis(ap=at[u][:, c:c + 1], axis=0),
                                    bounds_check=NPAD + EPAD - 1, oob_is_err=False).then_inc(gathered[u], 16)

                        def scatter(k, cs):
                            if 0 in cs:
                                freed(pool, f_scattered[k.par], 64 * k.half)
                                nc.gpsimd.tensor_copy(last[k.par][:, :], last_all[:, columns(k)]).then_inc(last_picked, 1)
                                pool.wait_ge(last_picked, k.n + 1)
                                pool.wait_ge(f_ready, k.n + 1)
                                pool.sem_inc(passed, 1)
                            for c in cs:
                                nc.gpsimd.indirect_dma_start(
                                    out=out[:, :], in_=or_[k.par][:, c, :], in_offset=None,
                                    out_offset=bass.IndirectOffsetOnAxis(ap=last[k.par][:, c:c + 1], axis=0),
                                    bounds_check=NPAD - 1, oob_is_err=False).then_inc(f_scattered[k.par], 16)

                        def ahead():
                            if s == 0:
                                find(Tile(0, 0))
                                find(Tile(0, 1))
                            gather(Tile(0, 0), range(CH))
                            if s == 0:
                                find(Tile(0, 2))
                            gather(Tile(0, 1), range(CH))

                        def body(i, j, k):
                            gathers = i is not None and (i + 2).exists()
                            scatters = final and k is not None and not (isinstance(k.n, int) and k.n == 0)
                            if gathers:
                                gather(i + 2, (0, 1))
                            if j is not None and keep_on_pool:
                                keep(pool, nc.gpsimd, j)
                            if s == 0 and i is not None and (i + 3).exists():
                                find(i + 3)
                            if gathers:
                                gather(i + 2, (2, 3))
                            if final and k is not None:
                                pool.wait_ge(ve_ready, k.n + 1)
                                freed(pool, f_ready, k.n - 1)
                                nc.gpsimd.tensor_tensor(rs_[k.par][:, :], ve_[:, :], minus_half[:, :], ALU.pow).then_inc(rs_ready, 1)
                                pool.wait_ge(rs_ready, 2 * k.n + 1)
                                nc.gpsimd.tensor_tensor(shift_[k.par][:, :], nm_[:, :], rs_[k.par][:, :], ALU.mult).then_inc(rs_ready, 1)
                            if scatters:
                                scatter(k + (-1), range(CH))

                        pipeline(pool, ahead, body)
                        if final:
                            scatter(Tile(ET // 2, 0), range(CH))
                            for u in range(2):
                                pool.wait_ge(f_scattered[u], 64 * OF_PARITY[u])

                    @block.scalar
                    def _(act):
                        def split_g(i):
                            act.wait_ge(gT_full, n + i.n + 1)
                            freed(act, t_full, KT * (n + i.n))
                            nc.scalar.activation(g_hi[:, :], gT_bank[:, :], ACT.Copy).then_inc(g_hi_ready, 1)

                        def out_rows(k):
                            freed(act, f_scattered[k.par], 64 * k.half)
                            act.wait_ge(rs_ready, 2 * k.n + 2)
                            for c in range(CH):
                                ins = nc.scalar.activation(or_[k.par][:, c, :], yo_[k.par][:, c, :], ACT.Identity,
                                                           bias=shift_[k.par][:, c:c + 1], scale=rs_[k.par][:, c:c + 1])
                            ins.then_inc(f_ready, 1)

                        def ahead():
                            split_g(Tile(0, 0))

                        def body(i, j, k):
                            if i is not None:
                                act.wait_ge(t_full, KT * (n + i.n) + 1)
                                freed(act, a_ready, n + i.n)
                                nc.scalar.activation(msg[:, :], t_bank[0][:, :], ACT.Identity, bias=b("et0")).then_inc(msg_ready, 1)
                            if j is not None:
                                act.wait_ge(r_full, n + j.n + 1)
                                freed(act, t1_ready, n + j.n)
                                nc.scalar.activation(r_[:, :], r_bank[:, :], ACT.Sigmoid, bias=b_r).then_inc(r_ready, 1)
                                act.wait_ge(z_full, n + j.n + 1)
                                freed(act, m_ready, n + j.n)
                                freed(act, zh_ready, n + j.n)
                                nc.scalar.activation(z_[:, :], z_bank[:, :], ACT.Sigmoid, bias=b_z).then_inc(z_ready, 1)
                            if i is not None:
                                u = i.par
                                act.wait_ge(h_loaded[u], 16 * (i.of_parity(s) + 1))
                                freed(act, z_full, n + i.n - 1)
                                nc.scalar.activation(h_hi[u][:, :], h[u][:, :], ACT.Copy).then_inc(h_hi_ready, 1)
                            if j is not None:
                                act.wait_ge(t2_ready, n + j.n + 1)
                                nc.scalar.activation(n_[:, :], t2_[:, :], ACT.Tanh, bias=b("ih_n")).then_inc(n_ready, 1)
                            if i is not None:
                                if (i + 1).exists():
                                    split_g(i + 1)
                            if final and k is not None and not (isinstance(k.n, int) and k.n == 0):
                                out_rows(k + (-1))
                            if j is not None and not final:
                                act.wait_ge(row_full, n + j.n + 1)
                                before = j + (-1)
                                freed(act, h_stored[before.par], 32 * (before.of_parity(s) + 1))
                                nc.scalar.activation(hrow[:, :, :].rearrange(flat), row_bank[:, :],
                                                     ACT.Copy).then_inc(hrow_ready, 1)
                            if i is not None:
                                act.wait_ge(a_ready, n + i.n + 1)
                                freed(act, z_full, n + i.n)
                                freed(act, a_lo_ready, n + i.n)
                                nc.scalar.activation(a_hi[:, :], a[:, :], ACT.Copy).then_inc(a_hi_ready, 1)
                            if j is not None and final:
                                act.wait_ge(gate_full, j.n + 1)
                                freed(act, fin_ready, j.n)
                                nc.scalar.activation(gate_[:, :, :].rearrange(flat), row_bank[:, :],
                                                     ACT.Sigmoid).then_inc(gate_ready, 1)

                        pipeline(act, ahead, body)
                        if final:
                            out_rows(Tile(ET // 2, 0))

                    @block.vector
                    def _(v):
                        def split_g(i):
                            v.wait_ge(g_hi_ready, n + i.n + 1)
                            freed(v, t_full, KT * (n + i.n))
                            nc.vector.tensor_tensor(g_lo[:, :], gT_bank[:, :], g_hi[:, :].bitcast(F32),
                                                    ALU.subtract).then_inc(g_lo_ready, 1)

                        def lay(i, kind):
                            v.wait_ge(msg_ready, KT * (n + i.n) + kind)
                            v.wait_ge(t_full, KT * (n + i.n) + kind + 1)
                            v.sem_inc(v_passed, 1)
                            nc.vector.copy_predicated(msg[:, :], mask[i.par][:, kind - 1, :],
                                                      t_bank[kind % 2][:, :]).then_inc(msg_ready, 1)

                        def ahead():
                            nc.vector.memset(acarry[:, :], 0.0).then_inc(acarry_ready, 1)
                            split_g(Tile(0, 0))

                        def body(i, j, k):
                            stage_c = final and k is not None
                            if stage_c:
                                v.wait_ge(gate_ready, k.n + 1)
                                v.wait_ge(j_full, k.n + 1)
                                nc.vector.tensor_tensor(fin_[:, :, :].rearrange(flat), in_bank[:, :],
                                                        gate_[:, :, :].rearrange(flat), ALU.mult).then_inc(fin_ready, 1)
                            if i is not None:
                                u = i.par
                                v.wait_ge(aux_loaded[u], 32 * (i.of_parity(s) + 1))
                                lay(i, 1)
                            if j is not None:
                                v.wait_ge(hn_full, n + j.n + 1)
                                v.wait_ge(r_ready, n + j.n + 1)
                                nc.vector.scalar_tensor_tensor(t1_[:, :], hn_bank[:, :], b("hh_n"), r_[:, :],
                                                               ALU.add, ALU.mult).then_inc(t1_ready, 1)
                                v.wait_ge(in_full, n + j.n + 1)
                                v.wait_ge(t1_ready, n + j.n + 1)
                                freed(v, n_ready, n + j.n)
                                nc.vector.tensor_tensor(t2_[:, :], in_bank[:, :], t1_[:, :], ALU.add).then_inc(t2_ready, 1)
                            if stage_c:
                                v.wait_ge(fin_ready, k.n + 1)
                                v.wait_ge(x1_loaded[k.par], 32 * (k.half + 1))
                                freed(v, f_ready, k.n - 1)
                                nc.vector.tensor_tensor(yo_[k.par][:, :, :], fin_[:, :, :], x1r[k.par][:, :, :], ALU.add).then_inc(yo_ready, 1)
                            if i is not None:
                                v.wait_ge(h_hi_ready, n + i.n + 1)
                                freed(v, z_full, n + i.n - 1)
                                nc.vector.tensor_tensor(h_lo[u][:, :], h[u][:, :], h_hi[u][:, :].bitcast(F32),
                                                        ALU.subtract).then_inc(h_lo_ready, 1)
                                lay(i, 2)
                            if j is not None:
                                v.wait_ge(n_ready, n + j.n + 1)
                                v.wait_ge(z_ready, n + j.n + 1)
                                nc.vector.scalar_tensor_tensor(m_[:, :], z_[:, :], 1.0, n_[:, :],
                                                               ALU.subtract, ALU.mult).then_inc(m_ready, 1)
                            if j is not None and not keep_on_pool:
                                keep(v, nc.vector, j)
                            if i is not None and (i + 1).exists():
                                split_g(i + 1)
                            if stage_c:
                                v.wait_ge(yo_ready, k.n + 1)
                                for c in range(CH):
                                    ins = nc.vector.bn_stats(st_[:, c, :], yo_[k.par][:, c, :])
                                ins.then_inc(f_stat, 1)
                            if j is not None:
                                v.wait_ge(m_ready, n + j.n + 1)
                                v.wait_ge(zh_ready, n + j.n + 1)
                                if final:
                                    freed(v, j_full, j.n - 1)
                                else:
                                    freed(v, h_stored[j.par], 32 * j.of_parity(s))
                                nc.vector.tensor_tensor(hn_[j.par][:, :], zh_[:, :], m_[:, :], ALU.subtract).then_inc(hn_ready, 1)
                            if stage_c:
                                v.wait_ge(f_stat, 2 * k.n + 1)
                                v.sem_inc(v_passed, 1)
                                for c in range(CH):
                                    ins = nc.vector.bn_aggr(mv_[:, c, :], st_[:, c, :])
                                ins.then_inc(f_stat, 1)
                                v.wait_ge(f_stat, 2 * k.n + 2)
                                freed(v, rs_ready, 2 * k.n)
                                nc.vector.tensor_scalar(nm_[:, :], mv_[:, :, 0], -1.0, None, ALU.mult)
                                nc.vector.tensor_scalar(ve_[:, :], mv_[:, :, 1], LN_EPS, None, ALU.add).then_inc(ve_ready, 1)
                            if i is not None:
                                lay(i, 3)
                                v.wait_ge(msg_ready, KT * (n + i.n) + KT)
                                v.wait_ge(acarry_ready, n + s + i.n + 1)
                                freed(v, a_hi_ready, n + i.n)
                                nc.vector.tensor_tensor_scan(a[:, :], same[u][:, :], msg[:, :], acarry[:, :],
                                                             ALU.mult, ALU.add).then_inc(a_ready, 1)
                                v.wait_ge(a_ready, n + i.n + 1)
                                nc.vector.tensor_copy(acarry[:, :], a[:, TILE - 1:TILE]).then_inc(acarry_ready, 1)
                                v.wait_ge(a_hi_ready, n + i.n + 1)
                                freed(v, z_full, n + i.n)
                                nc.vector.tensor_tensor(a_lo[:, :], a[:, :], a_hi[:, :].bitcast(F32),
                                                        ALU.subtract).then_inc(a_lo_ready, 1)

                        pipeline(v, ahead, body)

                    @block.tensor
                    def _(pe):
                        def transpose_g(i):
                            pe.wait_ge(gathered[i.par], 64 * (i.of_parity(s) + 1))
                            freed(pe, g_lo_ready, n + i.n)
                            flip(gT_bank, g[i.par]).then_inc(gT_full, 1)

                        def messages(i, kinds):
                            for kind in kinds:
                                if kind >= 2:
                                    pe.wait_ge(msg_ready, KT * (n + i.n) + kind - 1)
                                mm = product3(t_bank[kind % 2], f"et{kind}", g_hi, g_lo, True, kind == 0)
                                if kind:
                                    mm = bias_cols(t_bank[kind % 2][:, :], f"et{kind}")
                                mm.then_inc(t_full, 1)

                        def ahead():
                            transpose_g(Tile(0, 0))
                            pe.wait_ge(g_lo_ready, n + 1)
                            freed(pe, msg_ready, KT * n)
                            messages(Tile(0, 0), (0, 1))

                        def body(i, j, k):
                            if j is not None:
                                pe.wait_ge(a_lo_ready, n + j.n + 1)
                                product3(r_bank, "ih_r", a_hi, a_lo, False, True).then_inc(r_full, 1)
                                product3(z_bank, "ih_z", a_hi, a_lo, False, True).then_inc(z_full, 1)
                                freed(pe, t2_ready, n + j.n)
                                if final:
                                    freed(pe, fin_ready, j.n)
                                product3(in_bank, "ih_n", a_hi, a_lo, True, True).then_inc(in_full, 1)
                            if i is not None:
                                u = i.par
                                messages(i, (2, 3))
                                if (i + 1).exists():
                                    transpose_g(i + 1)
                                pe.wait_ge(h_lo_ready, n + i.n + 1)
                                freed(pe, r_ready, n + i.n)
                                product3(r_bank, "hh_r", h_hi[u], h_lo[u], True, False)
                                freed(pe, z_ready, n + i.n)
                                product3(z_bank, "hh_z", h_hi[u], h_lo[u], True, False)
                                freed(pe, t1_ready, n + i.n)
                                product3(hn_bank, "hh_n", h_hi[u], h_lo[u], True, True).then_inc(hn_full, 1)
                            if i is not None and (i + 1).exists():
                                pe.wait_ge(g_lo_ready, n + i.n + 2)
                                pe.wait_ge(msg_ready, KT * (n + i.n) + 3)
                                messages(i + 1, (0,))
                            if j is not None:
                                u = j.par
                                pe.wait_ge(hn_ready, n + j.n + 1)
                                if final:
                                    pe.wait_ge(x1_loaded[u], 32 * (j.half + 1))
                                    freed(pe, gate_ready, j.n)
                                    row_product(row_bank, [(hn_[u], "i_h"), (x1T[u], "i_x")], "i").then_inc(gate_full, 1)
                                    row_product(in_bank, [(hn_[u], "j")], "j").then_inc(j_full, 1)
                                else:
                                    freed(pe, hrow_ready, n + j.n)
                                    flip(row_bank, chunks(hn_[u][:, :])).then_inc(row_full, 1)
                            if i is not None and (i + 1).exists():
                                pe.wait_ge(msg_ready, KT * (n + i.n + 1))
                                messages(i + 1, (1,))

                        pipeline(pe, ahead, body)


def kernel(**inputs):
    import numpy as np
    import concourse.bacc as bacc
    from concourse.bass_utils import run_bass_kernel_spmd

    q = {k: np.asarray(v) for k, v in inputs.items()}
    x = np.zeros((NPAD, P), np.float32)
    x[:N] = q["x"]
    dst = np.full(EPAD + 2, N, np.int32)
    dst[0] = -1
    dst[1:E + 1] = q["dst"]
    src = np.full(EPAD, N, np.int32)
    src[:E] = q["src"]
    kind = np.zeros(EPAD, np.int32)
    kind[:E] = q["edge_type_4"]
    ef = np.zeros((EPAD, F_E), np.float32)
    ef[:E] = q["edge_attr_64"]

    def by_column(a):
        return np.ascontiguousarray(a.reshape(ECOL, P).T)

    def linear(a):
        return np.ascontiguousarray(a.reshape(P, ECOL))

    we = np.zeros((2 * P, P), np.float32)
    we[:P + F_E] = q["L0_gnn_W_edge"]
    wm, iw = q["L0_gnn_W_mlp"], q["L1_gnn_i_w"].T
    parts = [we[:P], we[P:], wm[:P], wm[P:]] + [q["L1_gnn_W_et"][k].T for k in range(KT)]
    parts += [q["L1_gnn_W_ih"][k * P:(k + 1) * P].T for k in range(3)]
    parts += [q["L1_gnn_W_hh"][k * P:(k + 1) * P].T for k in range(3)]
    parts += [iw[:P], iw[P:], q["L1_gnn_j_w"].T]
    cols = [q["L0_gnn_b_edge"]] + [q["L1_gnn_b_et"][k] for k in range(KT)]
    cols += [q["L1_gnn_b_ih"][k * P:(k + 1) * P] for k in range(3)]
    cols += [q["L1_gnn_b_hh"][k * P:(k + 1) * P] for k in range(3)]
    brows = [q["L0_gnn_b_mlp"], q["L1_gnn_i_b"], q["L1_gnn_j_b"]] + [q["L1_gnn_b_et"][k] for k in range(KT)]
    arrays = {
        "x_rows": x,
        "dst_lin": linear(dst[1:-1]), "prev_lin": linear(dst[:-2]), "type_lin": linear(kind),
        "dst_cols": by_column(dst[1:-1]), "next_cols": by_column(dst[2:]), "src_cols": by_column(src),
        "ef_t": np.ascontiguousarray(ef.T),
        "weights": np.ascontiguousarray(np.concatenate(parts, axis=1)),
        "biases": np.ascontiguousarray(np.stack(cols, axis=1)),
        "bias_rows": np.ascontiguousarray(np.concatenate(brows).reshape(1, -1)),
    }
    nc = bacc.Bacc("TRN2", target_bir_lowering=False, num_devices=1)
    args = [nc.dram_tensor(k, a.shape, mybir.dt.from_np(a.dtype), kind="ExternalInput").ap() for k, a in arrays.items()]
    out = nc.dram_tensor("out_rows", (NPAD, P), F32, kind="ExternalOutput").ap()
    build(nc, *args, out)
    r = run_bass_kernel_spmd(nc, [arrays], core_ids=[0])
    return r.results[0]["out_rows"][:N]
```
